# Optimizing a Trainium2 kernel written in Bass

```python
import numpy as np
import jax
import jax.numpy as jnp

def _softmax(x, axis=-1):
    return jax.nn.softmax(x, axis=axis)

def _gelu(x):
    return jax.nn.gelu(x, approximate=True)

def _silu(x):
    return jax.nn.silu(x)

def _sigmoid(x):
    return jax.nn.sigmoid(x)

def _layernorm(x, axis=-1, eps=1e-05):
    m = jnp.mean(x, axis=axis, keepdims=True)
    v = jnp.var(x, axis=axis, keepdims=True)
    return (x - m) / jnp.sqrt(v + eps)

def _scatter_add(tgt, idx, src, axis=0):
    return tgt.at[idx].add(src)

def _segment_sum(src, seg, n):
    return jax.ops.segment_sum(src, seg, n)
kernel_name = 'mk_metaformer_d2_conv_nhwc256_r4_bad007'

def setup_inputs(seed: int=0):
    np.random.seed(seed)
    _w = jnp.asarray

    def _rec_inputs():
        import jax
        import jax.numpy as jnp
        _gk = jax.random.key(seed)
        x = -0.000125 + 0.9999 * jax.random.normal(jax.random.fold_in(_gk, 1), (32, 16, 16, 64), jnp.float32)
        return x
    x = _rec_inputs()

    def _L0_conv_setup():
        import jax, jax.numpy as jnp
        import numpy as np
        B_, H_, W_, DM = (32, 16, 16, 64)
        D_INNER, D_STATE, NHEADS, HEADDIM = (128, 16, 8, 16)
        D_IN_PROJ = D_INNER + 2 * D_STATE + NHEADS
        key = jax.random.key(seed)
        ks = jax.random.split(key, 4)
        x = jax.random.normal(ks[0], (B_, H_, W_, DM), dtype=jnp.float32)
        W_in = jax.random.normal(ks[1], (DM, D_IN_PROJ), dtype=jnp.float32) * 0.05
        dt_bias = jax.random.normal(ks[2], (NHEADS,), dtype=jnp.float32)
        A_log = jax.random.uniform(ks[3], (NHEADS,), dtype=jnp.float32)
        D_param = jnp.ones((NHEADS,), dtype=jnp.float32)
        ln_gamma = jnp.ones((D_INNER,), dtype=jnp.float32)
        ln_beta = jnp.zeros((D_INNER,), dtype=jnp.float32)
        W_out = jax.random.normal(jax.random.fold_in(key, 7), (D_INNER, DM), dtype=jnp.float32) * 0.05
        return {'x': x, 'W_in': W_in, 'dt_bias': dt_bias, 'A_log': A_log, 'D_param': D_param, 'ln_gamma': ln_gamma, 'ln_beta': ln_beta, 'W_out': W_out}
    _L0_conv_all = _L0_conv_setup()
    _L0_conv_in = {k: v for k, v in _L0_conv_all.items() if k in ('W_in', 'dt_bias', 'A_log', 'D_param', 'ln_gamma', 'ln_beta', 'W_out')}
    del _L0_conv_all

    def _L0_ffn_setup():
        import jax, jax.numpy as jnp
        import numpy as np
        B, T, D, H, E = (16, 1024, 64, 128, 8)
        key = jax.random.key(seed)
        ks = jax.random.split(key, 5)
        x = jax.random.normal(ks[0], (B, T, D), dtype=jnp.float32)
        gate_w = jax.random.normal(ks[1], (D, E), dtype=jnp.float32) * 0.02
        gate_b = jnp.zeros((E,), dtype=jnp.float32)
        W1 = jax.random.normal(ks[2], (E, D, H), dtype=jnp.float32) * 0.02
        b1 = jnp.zeros((E, H), dtype=jnp.float32)
        W2 = jax.random.normal(ks[3], (E, H, D), dtype=jnp.float32) * 0.02
        b2 = jnp.zeros((E, D), dtype=jnp.float32)
        return {'x': x, 'gate_w': gate_w, 'gate_b': gate_b, 'W1': W1, 'b1': b1, 'W2': W2, 'b2': b2}
    _L0_ffn_all = _L0_ffn_setup()
    _L0_ffn_in = {k: v for k, v in _L0_ffn_all.items() if k in ('gate_w', 'gate_b', 'W1', 'b1', 'W2', 'b2')}
    del _L0_ffn_all

    def _L1_conv_setup():
        import jax, jax.numpy as jnp
        import numpy as np
        BETA_MIN = 1e-06
        key = jax.random.key(seed)
        ks = jax.random.split(key, 4)
        B, H, W, C = (32, 56, 56, 64)
        x = jax.random.normal(ks[0], (B, H, W, C), dtype=jnp.float32)
        gamma_k = jax.random.uniform(ks[1], (1, 1, 8, C), dtype=jnp.float32) * (1.0 / 16.0)
        gamma_s = jax.random.uniform(ks[2], (3, 3, C, 1), dtype=jnp.float32) * (1.0 / 16.0)
        beta = jax.random.uniform(ks[3], (C,), dtype=jnp.float32) * 1e-06
        beta_outside = jnp.zeros((C,), dtype=jnp.float32)
        gamma_outside = jnp.ones((C,), dtype=jnp.float32)
        return {'x': x, 'gamma_k': gamma_k, 'gamma_s': gamma_s, 'beta': beta, 'beta_outside': beta_outside, 'gamma_outside': gamma_outside, 'surround_dist': 1}
    _L1_conv_all = _L1_conv_setup()
    _L1_conv_in = {k: v for k, v in _L1_conv_all.items() if k in ('gamma_k', 'gamma_s', 'beta', 'beta_outside', 'gamma_outside')}
    del _L1_conv_all

    def _L1_ffn_setup():
        import jax, jax.numpy as jnp
        import numpy as np
        TOP_K = 2
        key = jax.random.key(seed)
        ks = jax.random.split(key, 4)
        B, L, D, H, E = (8, 1024, 64, 256, 8)
        s = 0.02
        return {'x': jax.random.normal(ks[0], (B, L, D), jnp.float32), 'Wg': jax.random.normal(ks[1], (D, E), jnp.float32) * s, 'bg': jnp.zeros((E,), jnp.float32), 'W1': jax.random.normal(ks[2], (E, D, H), jnp.float32) * s, 'b1': jnp.zeros((E, H), jnp.float32), 'W2': jax.random.normal(ks[3], (E, H, D), jnp.float32) * s, 'b2': jnp.zeros((E, D), jnp.float32)}
    _L1_ffn_all = _L1_ffn_setup()
    _L1_ffn_in = {k: v for k, v in _L1_ffn_all.items() if k in ('Wg', 'bg', 'W1', 'b1', 'W2', 'b2')}
    del _L1_ffn_all
    return {'x': x, 'L0_conv_W_in': _L0_conv_in['W_in'], 'L0_conv_dt_bias': _L0_conv_in['dt_bias'], 'L0_conv_A_log': _L0_conv_in['A_log'], 'L0_conv_D_param': _L0_conv_in['D_param'], 'L0_conv_ln_gamma': _L0_conv_in['ln_gamma'], 'L0_conv_ln_beta': _L0_conv_in['ln_beta'], 'L0_conv_W_out': _L0_conv_in['W_out'], 'L0_ffn_gate_w': _L0_ffn_in['gate_w'], 'L0_ffn_gate_b': _L0_ffn_in['gate_b'], 'L0_ffn_W1': _L0_ffn_in['W1'], 'L0_ffn_b1': _L0_ffn_in['b1'], 'L0_ffn_W2': _L0_ffn_in['W2'], 'L0_ffn_b2': _L0_ffn_in['b2'], 'L1_conv_gamma_k': _L1_conv_in['gamma_k'], 'L1_conv_gamma_s': _L1_conv_in['gamma_s'], 'L1_conv_beta': _L1_conv_in['beta'], 'L1_conv_beta_outside': _L1_conv_in['beta_outside'], 'L1_conv_gamma_outside': _L1_conv_in['gamma_outside'], 'L1_ffn_Wg': _L1_ffn_in['Wg'], 'L1_ffn_bg': _L1_ffn_in['bg'], 'L1_ffn_W1': _L1_ffn_in['W1'], 'L1_ffn_b1': _L1_ffn_in['b1'], 'L1_ffn_W2': _L1_ffn_in['W2'], 'L1_ffn_b2': _L1_ffn_in['b2']}

def reference(x, L0_conv_W_in, L0_conv_dt_bias, L0_conv_A_log, L0_conv_D_param, L0_conv_ln_gamma, L0_conv_ln_beta, L0_conv_W_out, L0_ffn_gate_w, L0_ffn_gate_b, L0_ffn_W1, L0_ffn_b1, L0_ffn_W2, L0_ffn_b2, L1_conv_gamma_k, L1_conv_gamma_s, L1_conv_beta, L1_conv_beta_outside, L1_conv_gamma_outside, L1_ffn_Wg, L1_ffn_bg, L1_ffn_W1, L1_ffn_b1, L1_ffn_W2, L1_ffn_b2):
    import jax
    import jax.numpy as jnp

    def _L0_conv_ref(x, W_in, dt_bias, A_log, D_param, ln_gamma, ln_beta, W_out):
        import jax, jax.numpy as jnp
        import numpy as np
        B_, H_, W_, DM = (32, 16, 16, 64)
        D_INNER, D_STATE, NHEADS, HEADDIM = (128, 16, 8, 16)
        D_IN_PROJ = D_INNER + 2 * D_STATE + NHEADS
        B, H, W, Dm = x.shape
        L = H * W
        u = x.reshape(B, L, Dm)
        A = -jnp.exp(A_log)
        xbcdt = u @ W_in
        x_ssm = xbcdt[..., :D_INNER]
        B_ssm = xbcdt[..., D_INNER:D_INNER + D_STATE]
        C_ssm = xbcdt[..., D_INNER + D_STATE:D_INNER + 2 * D_STATE]
        dt = jax.nn.softplus(xbcdt[..., D_INNER + 2 * D_STATE:] + dt_bias)
        V = x_ssm.reshape(B, L, NHEADS, HEADDIM)
        dA = dt * A
        V_scaled = V * dA[..., None]
        KV = jnp.einsum('bls,blhp->bhsp', B_ssm, V_scaled)
        y = jnp.einsum('bls,bhsp->blhp', C_ssm, KV)
        y = y + V * D_param[None, None, :, None]
        y = y.reshape(B, L, D_INNER)
        mu = jnp.mean(y, axis=-1, keepdims=True)
        var = jnp.var(y, axis=-1, keepdims=True)
        y = (y - mu) / jnp.sqrt(var + 1e-05) * ln_gamma + ln_beta
        out = y @ W_out
        return out.reshape(B, H, W, Dm)

    def _L0_ffn_ref(x, gate_w, gate_b, W1, b1, W2, b2):
        import jax, jax.numpy as jnp
        import numpy as np
        B, T, D, H, E = (16, 1024, 64, 128, 8)
        Bb, Tt, Dd = x.shape
        Ee = gate_w.shape[1]
        xf = x.reshape(-1, Dd)
        N = xf.shape[0]
        logits = xf @ gate_w + gate_b
        probs = jax.nn.softmax(logits, axis=-1)
        top2_vals, top2_idx = jax.lax.top_k(probs, 2)
        cw = jnp.zeros((N, Ee), dtype=xf.dtype).at[jnp.arange(N)[:, None], top2_idx].add(top2_vals)

        def step(acc, params):
            w1, bb1, w2, bb2, we = params
            h = jax.nn.gelu(xf @ w1 + bb1, approximate=False)
            y = h @ w2 + bb2
            return (acc + we[:, None] * y, None)
        out, _ = jax.lax.scan(step, jnp.zeros_like(xf), (W1, b1, W2, b2, cw.T))
        return out.reshape(Bb, Tt, Dd)

    def _L1_conv_ref(x, gamma_k, gamma_s, beta, beta_outside, gamma_outside, surround_dist):
        import jax, jax.numpy as jnp
        import numpy as np
        BETA_MIN = 1e-06
        B, H, W, C = x.shape
        G = C // 8
        x2 = x * x
        w = gamma_k[0, 0].reshape(8, G, 8)
        Pk = jnp.einsum('bhwgi,igo->bhwgo', x2.reshape(B, H, W, G, 8), w)
        Pk = Pk.reshape(B, H, W, C)
        mask = jnp.array([[1.0, 1.0, 1.0], [1.0, 0.0, 1.0], [1.0, 1.0, 1.0]], dtype=x.dtype)
        k = gamma_s[..., 0] * mask[:, :, None]
        kern = k[:, :, None, :]
        Ps = jax.lax.conv_general_dilated(x2, kern, window_strides=(1, 1), padding='SAME', rhs_dilation=(surround_dist, surround_dist), dimension_numbers=('NHWC', 'HWIO', 'NHWC'), feature_group_count=C)
        norm_pool = jnp.reciprocal(jnp.sqrt(Pk + Ps + (beta + BETA_MIN)))
        return x * norm_pool * gamma_outside + beta_outside

    def _L1_ffn_ref(x, Wg, bg, W1, b1, W2, b2):
        import jax, jax.numpy as jnp
        import numpy as np
        TOP_K = 2
        B, L, D = x.shape
        E = W1.shape[0]
        xf = x.reshape(-1, D)
        gate_logits = xf @ Wg + bg
        top_w, top_i = jax.lax.top_k(gate_logits, TOP_K)
        top_w = jax.nn.softmax(top_w, axis=-1)
        w_dense = jnp.sum(jax.nn.one_hot(top_i, E, dtype=xf.dtype) * top_w[..., None], axis=1)
        out = jnp.zeros_like(xf)
        for e in range(E):
            h = jax.nn.gelu(xf @ W1[e] + b1[e], approximate=False)
            out = out + w_dense[:, e:e + 1] * (h @ W2[e] + b2[e])
        return out.reshape(B, L, D)

    def _gn(v, G=32, eps=1e-05):
        B_, H_, W_, C_ = v.shape
        g = v.reshape(B_, H_, W_, G, C_ // G)
        m = jnp.mean(g, axis=(1, 2, 4), keepdims=True)
        s = jnp.var(g, axis=(1, 2, 4), keepdims=True)
        return ((g - m) / jnp.sqrt(s + eps)).reshape(v.shape)

    def _ln_c(v, eps=1e-06):
        m = jnp.mean(v, axis=-1, keepdims=True)
        s = jnp.var(v, axis=-1, keepdims=True)
        return (v - m) / jnp.sqrt(s + eps)

    def _ln_t(v, eps=1e-05):
        m = jnp.mean(v, axis=-1, keepdims=True)
        s = jnp.var(v, axis=-1, keepdims=True)
        return (v - m) / jnp.sqrt(s + eps)

    def _to_tokens(v):
        B_, H_, W_, C_ = v.shape
        return v.reshape(B_, H_ * W_, C_)

    def _from_tokens(t, like):
        return t.reshape(like.shape)
    x = x + _L0_conv_ref(_ln_c(x), L0_conv_W_in, L0_conv_dt_bias, L0_conv_A_log, L0_conv_D_param, L0_conv_ln_gamma, L0_conv_ln_beta, L0_conv_W_out)
    t = _to_tokens(x)
    t = t + _L0_ffn_ref(_ln_t(t), L0_ffn_gate_w, L0_ffn_gate_b, L0_ffn_W1, L0_ffn_b1, L0_ffn_W2, L0_ffn_b2)
    x = _from_tokens(t, x)
    x = x + _L1_conv_ref(_ln_c(x), L1_conv_gamma_k, L1_conv_gamma_s, L1_conv_beta, L1_conv_beta_outside, L1_conv_gamma_outside, 1)
    t = _to_tokens(x)
    t = t + _L1_ffn_ref(_ln_t(t), L1_ffn_Wg, L1_ffn_bg, L1_ffn_W1, L1_ffn_b1, L1_ffn_W2, L1_ffn_b2)
    x = _from_tokens(t, x)
    return x

_drawn_inputs = setup_inputs


def setup_inputs(seed=0):
    import zlib

    import numpy as np

    out = dict(_drawn_inputs(seed))
    spreads = {'L0_conv_D_param': (1.0, 0.6),
     'L0_conv_ln_gamma': (1.0, 0.2),
     'L0_conv_ln_beta': (0.0, 0.1),
     'L0_ffn_gate_b': (0.0, 0.451),
     'L0_ffn_b1': (0.0, 0.8),
     'L0_ffn_b2': (0.0, 0.431),
     'L1_conv_beta_outside': (0.0, 0.1),
     'L1_conv_gamma_outside': (1.0, 0.2),
     'L1_ffn_bg': (0.0, 0.371),
     'L1_ffn_b1': (0.0, 0.8),
     'L1_ffn_b2': (0.0, 0.305)}
    factors = {'L0_ffn_gate_w': 3.831,
     'L0_ffn_W1': 8.0,
     'L0_ffn_W2': 8.0,
     'L1_conv_beta': 8.0,
     'L1_ffn_W1': 8.0,
     'L1_ffn_W2': 6.999}
    for name, (base, spread) in spreads.items():
        noise = np.random.default_rng([zlib.crc32(name.encode()), seed]).standard_normal(out[name].shape)
        drawn = base * np.exp(spread * noise) if base else spread * noise
        out[name] = jnp.asarray(drawn.astype(out[name].dtype))
    for name, factor in factors.items():
        out[name] = (out[name] * factor).astype(out[name].dtype)
    return out
```

```python
from contextlib import ExitStack

import numpy as np

import concourse.bass as bass
from concourse import mybir

F32 = mybir.dt.float32
F16 = mybir.dt.float16
ACT = mybir.ActivationFunctionType
ALU = mybir.AluOpType
AX = mybir.AxisListType.X

P = 128
IMAGES, SIDE, C = 32, 16, 64
PIX = SIDE * SIDE
IPG = 4
GROUPS = IMAGES // IPG
TOK = IPG * PIX
T = TOK // P
HALF = TOK // 2
E = 8
PAIRS = E // 2
INNER, STATE, HEADS = 128, 16, 8
HDIM = INNER // HEADS
PROJ = INNER + 2 * STATE + HEADS
CHUNKS = (1, 2)
RING = 8
WS = 16.0


class Count:

    def __init__(self, sem, per):
        self.sem, self.per = sem, per

    def at(self, g, k=None):
        return g * self.per + (self.per if k is None else k)


def moe_order():
    order = []
    for cyc in range(-2, GROUPS):
        if 0 <= cyc + 2 < GROUPS:
            order.append((0, cyc + 2))
        if 0 <= cyc < GROUPS:
            order.append((1, cyc))
    return order


def build_metaformer(nc, x, W_in, dt_bias, A_log, D_param, ln_gamma, ln_beta, W_out, g0_w, g0_b, m0_W1, m0_b1,
                     m0_W2, m0_b2, gamma_k, gamma_s, beta, beta_out, gamma_out, g1_w, g1_b, m1_W1, m1_b1, m1_W2,
                     m1_b2, out):
    ORDER = moe_order()
    POS = {m: n for n, m in enumerate(ORDER)}
    CHUNK_BASE = {}
    n = 0
    for m in ORDER:
        CHUNK_BASE[m] = n
        n += E * CHUNKS[m[0]]

    with ExitStack() as ctx:
        def sb(name, shape, dt=F32):
            return ctx.enter_context(nc.sbuf_tensor(name, shape, dt))

        def psum(name, shape, dt=F32):
            return ctx.enter_context(nc.psum_tensor(name, shape, dt))

        def sem(name):
            return ctx.enter_context(nc.semaphore(name))

        def count(name, per):
            return Count(sem(name), per)

        ident16 = sb("ident16", [P, P], F16)
        ident32 = sb("ident32", [P, P])
        neg_half = sb("neg_half", [P, T])
        iota_m8 = sb("iota_m8", [P, E])
        win_f = sb("win_f", [P, PROJ])
        win = sb("win", [P, 2, PROJ], F16)
        wout_f = sb("wout_f", [P, C])
        wout_g = sb("wout_g", [P, C])
        wout = sb("wout", [P, 2, C], F16)
        gam_col = sb("gam_col", [P, 1])
        bet_col = sb("bet_col", [P, 1])
        bet_rep = sb("bet_rep", [P, P])
        out_bias = sb("out_bias", [P, C])
        dtb = sb("dtb", [P, HEADS])
        alog = sb("alog", [P, HEADS])
        expa = sb("expa", [P, HEADS])
        dpar = sb("dpar", [P, HEADS])
        gw_f = [sb(f"gw_f{l}", [P, E]) for l in range(2)]
        gw = [sb(f"gw{l}", [P, 2, E], F16) for l in range(2)]
        gb = [sb(f"gb{l}", [P, E]) for l in range(2)]
        NC = [E * c for c in CHUNKS]
        w1 = [sb(f"w1_{l}", [P, 2, NC[l], P], F16) for l in range(2)]
        w2 = [sb(f"w2_{l}", [P, NC[l], C]) for l in range(2)]
        b1 = [sb(f"b1_{l}", [P, NC[l]]) for l in range(2)]
        b2 = [sb(f"b2_{l}", [P, PAIRS]) for l in range(2)]
        mix = sb("mix", [P, P])
        taps = sb("taps", [P, 9])
        nbias = sb("nbias", [P, 1])
        bo_rep = sb("bo_rep", [P, C])
        go_col = sb("go_col", [P, 1])

        X0 = [sb(f"X0_{i}", [P, T, C]) for i in range(2)]
        X0b = sb("X0b", [P, T, C])
        X1 = [sb(f"X1_{i}", [P, T, C]) for i in range(2)]
        X2 = [sb(f"X2_{i}", [P, T, C]) for i in range(2)]
        X2b = sb("X2b", [P, T, C])
        X3 = [sb(f"X3_{i}", [P, T, C]) for i in range(2)]
        X4 = [sb(f"X4_{i}", [P, T, C]) for i in range(2)]
        FINT = sb("FINT", [P, T, C])
        xcen = sb("xcen", [P, T, C])
        xsq = sb("xsq", [P, T, C])
        xnrm = sb("xnrm", [P, T, C])
        xcen2 = sb("xcen2", [P, T, C])
        xsq2 = sb("xsq2", [P, T, C])
        xnrm2 = sb("xnrm2", [P, T, C])
        xsplit = sb("xsplit", [P, T, 2 * C], F16)
        xsplit2 = sb("xsplit2", [P, T, 2 * C], F16)
        stat = {L: sb(f"stat_{L}", [P, 4, T]) for L in "anbcd"}
        xTa = sb("xTa", [P, TOK], F16)
        xT = [[sb(f"xT{l}_{i}", [P, TOK], F16) for i in range(2)] for l in range(2)]
        proj = sb("proj", [P, T, PROJ])
        ctS = sb("ctS", [STATE, TOK])
        zdt = sb("zdt", [P, 5, T, HEADS])
        Vs = sb("Vs", [P, T, INNER])
        Yd = sb("Yd", [P, T, INNER])
        Yc = sb("Yc", [P, T, INNER])
        Ysq = Vs
        KVs = sb("KVs", [STATE, IPG * INNER])
        ysplit = sb("ysplit", [P, 2, T, INNER], F16)
        yT = sb("yT", [P, 2, TOK], F16)
        gt = [sb(f"gt{l}", [P, 12, T, E]) for l in range(2)]
        gs = [sb(f"gs{l}", [P, 6, T]) for l in range(2)]
        wgt = [sb(f"wgt{l}", [P, E, T]) for l in range(2)]
        wTs = [sb(f"wTs{l}", [E * T, P]) for l in range(2)]
        WB = [sb(f"WB{l}", [P, PAIRS, TOK]) for l in range(2)]
        H = sb("H", [P, RING, TOK])
        w1_f = H[:, 0:2, :].rearrange("p n h -> p (n h)")
        ACC = [sb(f"ACC{l}", [P, TOK]) for l in range(2)]
        YW = sb("YW", [P, 4, HALF])
        PAD = sb("PAD", [P, 2, SIDE + 2, SIDE + 2])
        nacc = sb("nacc", [P, 2, SIDE, SIDE])
        nlog = sb("nlog", [P, 2, SIDE, SIDE])
        nrs = sb("nrs", [P, 2, SIDE, SIDE])
        nrg = sb("nrg", [P, 2, SIDE, SIDE])
        zc = xsq2
        scratch = [[nc.dram_tensor(f"w_scratch{l}_{i}", [E, TOK], F32).ap() for i in range(2)] for l in range(2)]

        hP = [psum(f"hP{i}", [P, TOK]) for i in range(2)]
        yP = [psum(f"yP{i}", [P, HALF]) for i in range(2)]
        sA = psum("sA", [P, HALF])
        sC = psum("sC", [P, HALF])
        sA16 = sA[:, :].bitcast(F16)
        sC16 = sC[:, :].bitcast(F16)

        loaded = sem("weights_loaded")
        w1_loaded = [sem(f"w1_loaded{l}") for l in range(2)]
        mix_loaded = sem("mix_loaded")
        zeroed = sem("zeroed")
        ident_made = sem("ident_made")
        prep = sem("prep")
        prep_act = sem("prep_act")
        bias_mm = sem("bias_mm")
        x_loaded = [sem(f"x_loaded{i}") for i in range(2)]
        ln_v = {L: count(f"ln_v_{L}", 5) for L in "anbcd"}
        ln_s = {L: count(f"ln_s_{L}", 1) for L in "anbcd"}
        ln_p = {L: count(f"ln_p_{L}", 2) for L in "anbcd"}
        ln_lo = {L: count(f"ln_lo_{L}", 1) for L in "anbd"}
        tr = {L: count(f"tr_{L}", 2 if L == "n" else 1) for L in "anbd"}
        trS = {L: count(f"trS_{L}", 2 if L == "n" else 1) for L in "anbd"}
        pj = count("pj", IPG)
        pjS = count("pjS", IPG)
        ct = count("ct", 2)
        ctC = count("ctC", 2)
        dtv = count("dtv", 5)
        dts = count("dts", 2)
        vd = count("vd", 1)
        x0b = count("x0b", 1)
        kv = count("kv", 1)
        kvS = count("kvS", 1)
        ymm = count("ymm", 2)
        yv = count("yv", 2)
        omm = count("omm", 1)
        x1v = count("x1v", 1)
        gmm = [count(f"gmm{l}", 1) for l in range(2)]
        GV = 17
        gv = [count(f"gv{l}", GV) for l in range(2)]
        ge = [count(f"ge{l}", 1) for l in range(2)]
        wtr = [count(f"wtr{l}", 1) for l in range(2)]
        wts = [count(f"wts{l}", 1) for l in range(2)]
        w_out = [[sem(f"w_out{l}_{i}") for i in range(2)] for l in range(2)]
        w_in = [[sem(f"w_in{l}_{i}") for i in range(2)] for l in range(2)]
        x2b = count("x2b", 1)
        ctr = count("ctr", 1)
        sqT = count("sqT", 2)
        cmm = count("cmm", 1)
        tap = count("tap", 18 - 2)
        nact = count("nact", 2)
        nsc = count("nsc", 1)
        utr = count("utr", 1)
        cz = count("cz", 3)
        h_ready = sem("h_ready")
        gelu_done = sem("gelu_done")
        y_ready = sem("y_ready")
        scaled = sem("scaled")
        summed = sem("summed")
        ftr = sem("ftr")
        fin = sem("fin")
        x_stored = [sem(f"x_stored{i}") for i in range(2)]

        xd = x.rearrange("(g m) h w c -> g m (h w) c", m=IPG)
        od = out.rearrange("(g m) h w c -> g m (h w) c", m=IPG)

        def ring_free(m, s):
            if s < RING:
                m = ORDER[POS[m] - 1]
                s += E * CHUNKS[m[0]]
            return 8 * POS[m] + 2 * ((s - RING) // (2 * CHUNKS[m[0]])) + 2

        def grouped(dram, g):
            return dram[g].rearrange("m (p k) c -> p m (k c)", k=2)

        def tiled(ap):
            return ap[:, :, :].rearrange("p (m k) c -> p m (k c)", k=2)

        def per_tile(ap, width):
            return ap.unsqueeze(2).to_broadcast([P, T, width])

        def per_col(ap, n, width):
            return ap.unsqueeze(1).to_broadcast([P, n, width])

        LN = {
            "a": dict(x=X0, c=xcen, q=xsq, n=xnrm, s=xsplit, w=C, eps=1e-6),
            "b": dict(x=X1, c=xcen, q=xsq, n=xnrm, s=xsplit, w=C, eps=1e-5),
            "c": dict(x=X2, c=xcen2, q=xsq2, n=xnrm2, s=None, w=C, eps=1e-6),
            "d": dict(x=X3, c=xcen2, q=xsq2, n=xnrm2, s=xsplit2, w=C, eps=1e-5),
            "n": dict(x=(Yd, Yd), c=Yc, q=Ysq, n=Yc, s=None, w=INNER, eps=1e-5),
        }

        def parts(L):
            if L == "n":
                return ysplit[:, 0], ysplit[:, 1]
            s = LN[L]["s"]
            return s[:, :, 0:C], s[:, :, C:2 * C]

        ctx.enter_context(nc.allow_non_contiguous_dma(reason="a few small constants are laid out per channel"))
        block = ctx.enter_context(nc.Block())

        AB_STEPS, CD_STEPS = 26, 17

        def walk(moe, ab, cd):
            def side(fn, g, steps, at, end):
                for k in range(steps * at // end, steps * (at + 1) // end):
                    fn(g, k)
            for k in range(AB_STEPS):
                ab(0, k)
            for cyc in range(-2, GROUPS):
                todo = [m for m in ((0, cyc + 2), (1, cyc)) if 0 <= m[1] < GROUPS]
                slots = [(m, s) for m in todo for s in range(E * CHUNKS[m[0]] + 2 * CHUNKS[m[0]] + 2)]
                end = len(slots)
                for at, (m, s) in enumerate(slots):
                    moe(m, s)
                    if 0 <= cyc + 3 < GROUPS:
                        side(ab, cyc + 3, AB_STEPS, at, end)
                    if 0 <= cyc + 1 < GROUPS:
                        side(cd, cyc + 1, CD_STEPS, at, end)

        @block.sync
        def _(sp):
            def rep(ap):
                return ap.partition_broadcast(P)

            sp.dma_start(tiled(X0[0]), grouped(xd, 0)).then_inc(x_loaded[0], 16)
            n_loads = 0
            for half in range(2):
                q = slice(half * C, half * C + C)
                for dst, src in ((win_f[q, :], W_in), (gw_f[0][q, :], g0_w), (gw_f[1][q, :], g1_w),
                                 (taps[q, :], gamma_s.rearrange("a b c o -> c (a b o)")),
                                 (nbias[q, :], beta.rearrange("(c o) -> c o", o=1)),
                                 (go_col[q, :], gamma_out.rearrange("(c o) -> c o", o=1)),
                                 (b2[0][q, :], m0_b2.rearrange("(j a) f -> a f j", a=2)[half]),
                                 (b2[1][q, :], m1_b2.rearrange("(j a) f -> a f j", a=2)[half])):
                    sp.dma_start(dst, src).then_inc(loaded, 16)
                    n_loads += 1
            for dst, src in ((wout_f[:, :], W_out), (gam_col[:, :], ln_gamma.rearrange("(c o) -> c o", o=1)),
                             (bet_col[:, :], ln_beta.rearrange("(c o) -> c o", o=1)),
                             (dtb[:, :], rep(dt_bias)), (alog[:, :], rep(A_log)), (dpar[:, :], rep(D_param)),
                             (gb[0][:, :], rep(g0_b)), (gb[1][:, :], rep(g1_b)), (bo_rep[:, :], rep(beta_out)),
                             (b1[0][:, :], m0_b1.rearrange("e h -> h e")),
                             (b1[1][:, :], m1_b1.rearrange("e (c h) -> h (e c)", h=P)),
                             (w2[0][:, :, :], m0_W2.rearrange("e h f -> h e f")),
                             (w2[1][:, :, :], m1_W2.rearrange("e (c h) f -> h (e c) f", h=P))):
                sp.dma_start(dst, src).then_inc(loaded, 16)
                n_loads += 1
            assert n_loads == N_LOADS
            for half in range(2):
                sp.dma_start(w1_f[half * C:half * C + C, 0:NC[0] * P].rearrange("d (e h) -> d e h", e=E),
                             m0_W1.rearrange("e d h -> d e h")).then_inc(w1_loaded[0], 16)
            sp.wait_ge(zeroed, 2)
            gk = gamma_k.rearrange("a b i o -> (a b i) o")
            for half in range(2):
                for grp in range(8):
                    r = half * C + grp * 8
                    sp.dma_start(mix[r:r + 8, r:r + 8], gk[:, grp * 8:grp * 8 + 8]).then_inc(mix_loaded, 16)
            sp.wait_ge(prep, PREP_W1_0)
            for half in range(2):
                sp.dma_start(w1_f[half * C:half * C + C, :].rearrange("d (e h) -> d e h", e=E),
                             m1_W1.rearrange("e d h -> d e h")).then_inc(w1_loaded[1], 16)

            def spread_weights(l, g):
                i = g % 2
                sp.wait_ge(wts[l].sem, wts[l].at(g))
                sp.dma_start(scratch[l][i].rearrange("e (t p) -> (e t) p", p=P), wTs[l][:, :]).then_inc(w_out[l][i], 16)
                sp.wait_ge(w_out[l][i], 16 * (g // 2 + 1))
                if g >= 1:
                    sp.wait_ge(scaled, 8 * (POS[(l, g - 1)] + 1))
                for a in range(2):
                    src = scratch[l][i].rearrange("(j a) n -> a j n", a=2)[a]
                    sp.dma_start(WB[l][a * C:a * C + C, :, :], src.partition_broadcast(C)).then_inc(w_in[l][i], 16)

            def ab(g, k):
                if k == 0 and g + 1 < GROUPS:
                    if g >= 1:
                        sp.wait_ge(x0b.sem, x0b.at(g - 1))
                        sp.wait_ge(ln_v["a"].sem, ln_v["a"].at(g - 1, 2))
                    sp.dma_start(tiled(X0[(g + 1) % 2]), grouped(xd, g + 1)).then_inc(x_loaded[(g + 1) % 2], 16)
                if k == AB_STEPS - 1:
                    spread_weights(0, g)

            def cd(g, k):
                if k == CD_STEPS - 1:
                    spread_weights(1, g)

            def moe(m, s):
                l, g = m
                if l == 1 and s == E * CHUNKS[1] + 2 * CHUNKS[1] + 1:
                    sp.wait_ge(fin, 4 * (POS[m] + 1))
                    sp.dma_start(grouped(od, g), tiled(X4[g % 2])).then_inc(x_stored[g % 2], 16)

            walk(moe, ab, cd)
            for i in range(2):
                sp.wait_ge(x_stored[i], 16 * (GROUPS // 2))


        @block.gpsimd
        def _(pool):
            pool.memset(ident16[:, :], 0.0).then_inc(ident_made, 1)
            pool.memset(ident32[:, :], 0.0).then_inc(ident_made, 1)
            pool.wait_ge(ident_made, 2)
            for m in (ident16, ident32):
                pool.affine_select(out=m[:, :], in_=m[:, :], compare_op=ALU.not_equal, fill=1.0, base=0,
                                   pattern=[[-1, P]], channel_multiplier=1).then_inc(ident_made, 1)

            def variance(L, g):
                d, st = LN[L], stat[L]
                pool.wait_ge(ln_v[L].sem, ln_v[L].at(g, 3))
                pool.tensor_scalar(st[:, 2, :], st[:, 1, :], 1.0 / d["w"], d["eps"], ALU.mult, ALU.add)\
                    .then_inc(ln_p[L].sem, 1)
                pool.wait_ge(ln_p[L].sem, ln_p[L].at(g, 1))
                pool.tensor_tensor(st[:, 3, :], st[:, 2, :], neg_half[:, :], ALU.pow).then_inc(ln_p[L].sem, 1)

            def lo_part(L, g):
                hi, lo = parts(L)
                pool.wait_ge(ln_v[L].sem, ln_v[L].at(g, 5))
                pool.tensor_tensor(lo, LN[L]["n"][:, :, :], hi, ALU.subtract).then_inc(ln_lo[L].sem, 1)

            def ab(g, k):
                if k == 1:
                    variance("a", g)
                elif k == 2:
                    lo_part("a", g)
                elif k == 9:
                    pool.wait_ge(pjS.sem, pjS.at(g))
                    if g == 0:
                        pool.wait_ge(prep, PREP_ALL)
                    else:
                        pool.wait_ge(ln_v["n"].sem, ln_v["n"].at(g - 1, 2))
                    pool.tensor_tensor(Yd[:, :, :].rearrange("p t (h d) -> p t h d", h=HEADS),
                                       proj[:, :, 0:INNER].rearrange("p t (h d) -> p t h d", h=HEADS),
                                       dpar[:, :].unsqueeze(1).unsqueeze(3).to_broadcast([P, T, HEADS, HDIM]),
                                       ALU.mult).then_inc(vd.sem, 1)
                    if g >= 1:
                        pool.wait_ge(x1v.sem, x1v.at(g - 1))
                    pool.wait_ge(x_loaded[g % 2], 16 * (g // 2 + 1))
                    pool.tensor_tensor(X0b[:, :, :], X0[g % 2][:, :, :], per_col(out_bias[:, :], T, C), ALU.add)\
                        .then_inc(x0b.sem, 1)
                elif k == 14:
                    variance("n", g)
                elif k == 15:
                    lo_part("n", g)
                elif k == 20:
                    variance("b", g)
                elif k == 21:
                    lo_part("b", g)

            def cd(g, k):
                if k == 1:
                    variance("c", g)
                elif k == 2:
                    if g >= 1:
                        pool.wait_ge(cz.sem, cz.at(g - 1))
                    pool.wait_ge(fin, 4 * (POS[(0, g)] + 1))
                    pool.tensor_tensor(X2b[:, :, :], X2[g % 2][:, :, :], per_col(bo_rep[:, :], T, C), ALU.add)\
                        .then_inc(x2b.sem, 1)
                elif k == 7:
                    pool.wait_ge(nact.sem, nact.at(g, 2))
                    pool.tensor_scalar(nrg[:, :, :, :], nrs[:, :, :, :], go_col[:, 0:1], None, ALU.mult)\
                        .then_inc(nsc.sem, 1)
                elif k == 11:
                    variance("d", g)
                elif k == 12:
                    lo_part("d", g)

            def moe(m, s):
                l, g = m
                ch = CHUNKS[l]
                n = s - 2 * ch - ch - 1
                if n >= 0 and n % ch == 0 and n // ch < 2 * PAIRS:
                    u = n // ch
                    j, hf = u // 2, u % 2
                    if j >= 1:
                        pool.wait_ge(scaled, 8 * POS[m] + u + 1)
                        if j >= 2:
                            pool.wait_ge(summed, 6 * POS[m] + u - 3)
                        pool.tensor_tensor(ACC[l][:, hf * HALF:(hf + 1) * HALF], ACC[l][:, hf * HALF:(hf + 1) * HALF],
                                           YW[:, u % 4, :], ALU.add).then_inc(summed, 1)

            walk(moe, ab, cd)

        @block.scalar
        def _(act):
            act.wait_ge(loaded, 16 * N_LOADS)
            nc.scalar.activation(expa[:, :], alog[:, :], ACT.Exp).then_inc(prep_act, 1)

            def squares(L, g):
                d = LN[L]
                act.wait_ge(ln_v[L].sem, ln_v[L].at(g, 2))
                nc.scalar.activation(d["q"][:, :, :], d["c"][:, :, :], ACT.Square).then_inc(ln_s[L].sem, 1)

            def evacuate_T(L, g, src, dst, k=None):
                act.wait_ge(tr[L].sem, tr[L].at(g, k))
                nc.scalar.activation(dst, src, ACT.Copy).then_inc(trS[L].sem, 1)

            def gate_exp(l, g):
                act.wait_ge(gv[l].sem, gv[l].at(g, 3))
                nc.scalar.activation(gt[l][:, 2], gt[l][:, 1], ACT.Exp).then_inc(ge[l].sem, 1)

            def gate_evac(l, g, src):
                act.wait_ge(wtr[l].sem, wtr[l].at(g))
                if g >= 1:
                    act.wait_ge(w_out[l][(g - 1) % 2], 16 * ((g - 1) // 2 + 1))
                nc.scalar.activation(wTs[l][:, :], src[0:E * T, 0:P], ACT.Copy).then_inc(wts[l].sem, 1)

            def ab(g, k):
                if k == 0:
                    squares("a", g)
                elif k == 3:
                    evacuate_T("a", g, sA16, xTa[:, :])
                elif 4 <= k < 8:
                    m = k - 4
                    act.wait_ge(pj.sem, pj.at(g, m + 1))
                    nc.scalar.activation(proj[:, 2 * m:2 * m + 2, :],
                                         sA[:, 0:2 * PROJ].rearrange("p (t n) -> p t n", t=2), ACT.Copy,
                                         scale=1.0 / WS).then_inc(pjS.sem, 1)
                elif k in (8, 10):
                    hf = (k - 8) // 2
                    act.wait_ge(ct.sem, ct.at(g, hf + 1))
                    nc.scalar.activation(ctS[:, hf * HALF:(hf + 1) * HALF], sA[0:STATE, :], ACT.Copy,
                                         scale=1.0 / WS).then_inc(ctC.sem, 1)
                elif k == 9:
                    act.wait_ge(dtv.sem, dtv.at(g, 2))
                    nc.scalar.activation(zdt[:, 2], zdt[:, 1], ACT.Exp).then_inc(dts.sem, 1)
                    act.wait_ge(dts.sem, dts.at(g, 1))
                    nc.scalar.activation(zdt[:, 3], zdt[:, 2], ACT.Ln, bias=1.0).then_inc(dts.sem, 1)
                elif k == 11:
                    act.wait_ge(kv.sem, kv.at(g))
                    nc.scalar.activation(KVs[:, :], sA[0:STATE, :], ACT.Copy).then_inc(kvS.sem, 1)
                elif k == 13:
                    squares("n", g)
                elif k in (16, 17):
                    hl = k - 16
                    evacuate_T("n", g, sA16, yT[:, hl, :], hl + 1)
                elif k == 19:
                    squares("b", g)
                elif k == 22:
                    if g >= 2:
                        act.wait_ge(h_ready, CHUNK_BASE[(0, g - 2)] + E)
                    evacuate_T("b", g, sA16, xT[0][g % 2][:, :])
                elif k == 24:
                    gate_exp(0, g)
                elif k == 25:
                    gate_evac(0, g, sA)

            def cd(g, k):
                if k == 0:
                    squares("c", g)
                elif k == 3:
                    act.wait_ge(ctr.sem, ctr.at(g))
                    if g == 0:
                        act.wait_ge(zeroed, 2)
                    for q in range(2):
                        nc.scalar.activation(
                            PAD[:, q, 1:SIDE + 1, 1:SIDE + 1].rearrange("p r (c k) -> p k r c", k=2),
                            sC[:, q * 256:(q + 1) * 256].rearrange("p (k r c) -> p k r c", k=2, c=SIDE // 2),
                            ACT.Square).then_inc(sqT.sem, 1)
                elif k == 6:
                    act.wait_ge(tap.sem, tap.at(g))
                    nc.scalar.activation(nlog[:, :, :, :], nacc[:, :, :, :], ACT.Ln).then_inc(nact.sem, 1)
                    act.wait_ge(nact.sem, nact.at(g, 1))
                    nc.scalar.activation(nrs[:, :, :, :], nlog[:, :, :, :], ACT.Exp, scale=-0.5).then_inc(nact.sem, 1)
                elif k == 10:
                    squares("d", g)
                elif k == 13:
                    if g >= 2:
                        act.wait_ge(h_ready, CHUNK_BASE[(1, g - 2)] + 2 * E)
                    evacuate_T("d", g, sC16, xT[1][g % 2][:, :])
                elif k == 15:
                    gate_exp(1, g)
                elif k == 16:
                    gate_evac(1, g, sC)

            def moe(m, s):
                l, g = m
                ch = CHUNKS[l]
                if s < E * ch:
                    n = CHUNK_BASE[m] + s
                    act.wait_ge(h_ready, n + 1)
                    if n == 0:
                        act.wait_ge(prep, PREP_ALL)
                    if n >= RING:
                        act.wait_ge(y_ready, ring_free(m, s))
                    j, r = s // (2 * ch), s % (2 * ch)
                    c, a = r // 2, r % 2
                    e = 2 * j + a
                    nc.scalar.activation(H[:, s % RING, :], hP[s % 2][:, :], ACT.Gelu,
                                         bias=b1[l][:, e * ch + c:e * ch + c + 1], scale=1.0 / WS)\
                        .then_inc(gelu_done, 1)

            walk(moe, ab, cd)

        @block.tensor
        def _(pe):
            pe.wait_ge(prep, PREP_ALL)
            pe.wait_ge(ident_made, 4)
            nc.tensor.matmul(sA[:, 0:C], bet_rep[:, :], wout_f[:, :], start=True, stop=True).then_inc(bias_mm, 1)

            def transposes16(L, g, dst, src, after, k=None):
                for sm, v in after:
                    pe.wait_ge(sm, v)
                for t in range(T):
                    mm = nc.tensor.transpose(dst[:, t * P:(t + 1) * P], src(t), ident16[:, :])
                mm.then_inc(tr[L].sem, 1)

            def gate_product(l, g, ps, src):
                pe.wait_ge(trS[("b", "d")[l]].sem, trS[("b", "d")[l]].at(g))
                for t in range(T):
                    for s in range(2):
                        mm = nc.tensor.matmul(ps[:, t * E:(t + 1) * E], src[:, t * P:(t + 1) * P], gw[l][:, s, :],
                                              start=(s == 0), stop=(s == 1))
                mm.then_inc(gmm[l].sem, 1)

            def gate_transpose(l, g, ps):
                pe.wait_ge(gv[l].sem, gv[l].at(g))
                nc.tensor.transpose(ps[0:E * T, 0:P], wgt[l][:, :, :], ident32[:, :]).then_inc(wtr[l].sem, 1)

            def ab(g, k):
                if k == 3:
                    if g == 0:
                        after = [(prep, PREP_BIAS)]
                    else:
                        after = [(wts[0].sem, wts[0].at(g - 1))]
                    transposes16("a", g, sA16, lambda t: xsplit[:, t, :],
                                 after + [(ln_lo["a"].sem, ln_lo["a"].at(g))])
                elif 4 <= k < 8:
                    m = k - 4
                    if m == 0:
                        pe.wait_ge(trS["a"].sem, trS["a"].at(g))
                    else:
                        pe.wait_ge(pjS.sem, pjS.at(g, m))
                    for t in range(2):
                        col = (2 * m + t) * P
                        for s in range(2):
                            mm = nc.tensor.matmul(sA[:, t * PROJ:(t + 1) * PROJ], xTa[:, col:col + P], win[:, s, :],
                                                  start=(s == 0), stop=(s == 1))
                    mm.then_inc(pj.sem, 1)
                elif k in (8, 10):
                    hf = (k - 8) // 2
                    if hf == 0:
                        pe.wait_ge(pjS.sem, pjS.at(g))
                    else:
                        pe.wait_ge(ctC.sem, ctC.at(g, 1))
                    for s in range(2):
                        mm = nc.tensor.matmul(sA[0:STATE, :], win[:, s, INNER + STATE:INNER + 2 * STATE],
                                              xTa[:, hf * HALF:(hf + 1) * HALF], start=(s == 0), stop=(s == 1))
                    mm.then_inc(ct.sem, 1)
                elif k == 11:
                    pe.wait_ge(ctC.sem, ctC.at(g))
                    pe.wait_ge(dtv.sem, dtv.at(g))
                    for m in range(IPG):
                        for t in range(2):
                            mm = nc.tensor.matmul(sA[0:STATE, m * INNER:(m + 1) * INNER],
                                                  proj[:, 2 * m + t, INNER:INNER + STATE], Vs[:, 2 * m + t, :],
                                                  start=(t == 0), stop=(t == 1))
                    mm.then_inc(kv.sem, 1)
                elif k in (12, 13):
                    hf = k - 12
                    if hf == 0:
                        pe.wait_ge(kvS.sem, kvS.at(g))
                    else:
                        pe.wait_ge(yv.sem, yv.at(g, 1))
                    for t in range(4):
                        tt = 4 * hf + t
                        mm = nc.tensor.matmul(sA[:, t * INNER:(t + 1) * INNER], ctS[:, tt * P:(tt + 1) * P],
                                              KVs[:, (tt // 2) * INNER:(tt // 2 + 1) * INNER], start=True, stop=True)
                    mm.then_inc(ymm.sem, 1)
                elif k in (16, 17):
                    hl = k - 16
                    if hl == 0:
                        after = [(ln_v["n"].sem, ln_v["n"].at(g, 5))]
                    else:
                        after = [(ln_lo["n"].sem, ln_lo["n"].at(g)),
                                 (trS["n"].sem, trS["n"].at(g, 1))]
                    transposes16("n", g, sA16, lambda t: ysplit[:, hl, t, :], after)
                elif k == 18:
                    pe.wait_ge(trS["n"].sem, trS["n"].at(g))
                    for t in range(T):
                        for n in range(4):
                            mm = nc.tensor.matmul(sA[:, t * C:(t + 1) * C], yT[:, n // 2, t * P:(t + 1) * P],
                                                  wout[:, n % 2, :], start=(n == 0), stop=(n == 3))
                    mm.then_inc(omm.sem, 1)
                elif k == 22:
                    transposes16("b", g, sA16, lambda t: xsplit[:, t, :],
                                 [(ln_lo["b"].sem, ln_lo["b"].at(g))])
                elif k == 23:
                    gate_product(0, g, sA, xT[0][g % 2])
                elif k == 25:
                    gate_transpose(0, g, sA)

            def cd(g, k):
                if k == 3:
                    if g >= 1:
                        pe.wait_ge(wts[1].sem, wts[1].at(g - 1))
                    else:
                        pe.wait_ge(mix_loaded, 16 * 16)
                    pe.wait_ge(ln_v["c"].sem, ln_v["c"].at(g))
                    for n in range(4):
                        mm = nc.tensor.transpose(sC[:, n * P:(n + 1) * P], xnrm2[:, 2 * n:2 * n + 2, :], ident32[:, :])
                    mm.then_inc(ctr.sem, 1)
                elif k == 4:
                    pe.wait_ge(sqT.sem, sqT.at(g))
                    nc.tensor.matmul(sC[:, :].rearrange("p (q r c) -> p q r c", q=2, r=SIDE), mix[:, :],
                                     PAD[:, :, 1:SIDE + 1, 1:SIDE + 1], start=True, stop=True).then_inc(cmm.sem, 1)
                elif k == 8:
                    pe.wait_ge(nsc.sem, nsc.at(g))
                    for q in range(2):
                        for kk in range(2):
                            src = nrg[:, q, :, :].rearrange("p r c -> p (r c)")[:, kk::2]
                            n = 2 * q + kk
                            mm = nc.tensor.transpose(sC[:, n * P:(n + 1) * P], src, ident32[:, :])
                    mm.then_inc(utr.sem, 1)
                elif k == 13:
                    transposes16("d", g, sC16, lambda t: xsplit2[:, t, :],
                                 [(ln_lo["d"].sem, ln_lo["d"].at(g))])
                elif k == 14:
                    gate_product(1, g, sC, xT[1][g % 2])
                elif k == 16:
                    gate_transpose(1, g, sC)

            def moe(m, s):
                l, g = m
                ch = CHUNKS[l]
                if s < E * ch:
                    n = CHUNK_BASE[m] + s
                    if s == 0:
                        pe.wait_ge(trS["bd"[l]].sem, trS["bd"[l]].at(g))
                    if n >= 2:
                        pe.wait_ge(gelu_done, n - 1)
                    j, r = s // (2 * ch), s % (2 * ch)
                    c, a = r // 2, r % 2
                    w = (2 * j + a) * ch + c
                    for sp in range(2):
                        for hf in range(2):
                            mm = nc.tensor.matmul(hP[s % 2][:, hf * HALF:(hf + 1) * HALF], w1[l][:, sp, w, :],
                                                  xT[l][g % 2][:, hf * HALF:(hf + 1) * HALF],
                                                  start=(sp == 0), stop=(sp == 1))
                    mm.then_inc(h_ready, 1)
                n = s - 2 * ch
                if 0 <= n < E * ch:
                    j, r = n // (2 * ch), n % (2 * ch)
                    hf, c = r // ch, r % ch
                    pe.wait_ge(gelu_done, CHUNK_BASE[m] + 2 * ch * j + 2 * c + 2)
                    if c == 0:
                        u = 8 * POS[m] + 2 * j + hf
                        if j >= 1:
                            pe.wait_ge(scaled, u - 1)
                        elif POS[m] >= 1:
                            pe.wait_ge(fin, 4 * POS[m])
                    for a in range(2):
                        mm = nc.tensor.matmul(yP[hf][a * C:(a + 1) * C, :], w2[l][:, (2 * j + a) * ch + c, :],
                                              H[:, (2 * ch * j + 2 * c + a) % RING, hf * HALF:(hf + 1) * HALF],
                                              start=(c == 0), stop=(c == ch - 1))
                    if c == ch - 1:
                        mm.then_inc(y_ready, 1)
                if s == E * ch + 2 * ch + 1:
                    for hf in range(2):
                        pe.wait_ge(summed, 6 * POS[m] + 5 + hf)
                        pe.wait_ge(scaled, 8 * (POS[m] + 1))
                        for t in range(4):
                            col = (4 * hf + t) * P
                            mm = nc.tensor.transpose(yP[hf][:, t * P:(t + 1) * P], ACC[l][:, col:col + P], ident32[:, :])
                        mm.then_inc(ftr, 1)

            walk(moe, ab, cd)

        @block.vector
        def _(dve):
            v = nc.vector
            steps = [0]

            def did(ins):
                ins.then_inc(prep, 1)
                steps[0] += 1

            v.memset(PAD[:, :, :, :], 0.0).then_inc(zeroed, 1)
            v.memset(mix[:, :], 0.0).then_inc(zeroed, 1)
            did(v.memset(neg_half[:, :], -0.5))
            for e in range(E):
                m = v.memset(iota_m8[:, e:e + 1], float(e - E))
            did(m)
            dve.wait_ge(w1_loaded[0], 32)
            n0 = NC[0] * P
            flat = [w1[l][:, :, :, :].rearrange("p s n h -> p s (n h)") for l in range(2)]

            def split(dst_hi, dst_lo, src):
                did(v.tensor_scalar(dst_hi, src, WS, None, ALU.mult))
                dve.wait_ge(prep, steps[0])
                did(v.scalar_tensor_tensor(out=dst_lo, in0=src, scalar=WS, in1=dst_hi, op0=ALU.mult,
                                           op1=ALU.subtract))

            split(flat[0][:, 0], flat[0][:, 1], w1_f[:, 0:n0])
            dve.wait_ge(loaded, 16 * N_LOADS)
            did(v.tensor_scalar(wout_g[:, :], wout_f[:, :], gam_col[:, 0:1], None, ALU.mult))
            did(v.tensor_scalar(bet_rep[:, :], w1_f[:, 0:P], 0.0, bet_col[:, 0:1], ALU.mult, ALU.add))
            dve.wait_ge(prep, steps[0])
            split(wout[:, 0, :], wout[:, 1, :], wout_g[:, :])
            split(win[:, 0, :], win[:, 1, :], win_f[:, :])
            split(gw[0][:, 0, :], gw[0][:, 1, :], gw_f[0][:, :])
            assert steps[0] == PREP_W1_0
            split(gw[1][:, 0, :], gw[1][:, 1, :], gw_f[1][:, :])
            did(v.tensor_scalar(nbias[:, :], nbias[:, :], 1e-6, None, ALU.add))
            dve.wait_ge(w1_loaded[1], 32)
            split(flat[1][:, 0], flat[1][:, 1], w1_f[:, :])
            assert steps[0] == PREP_ALL_
            dve.wait_ge(bias_mm, 1)
            did(v.tensor_copy(out_bias[:, :], sA[:, 0:C]))
            assert steps[0] == PREP_BIAS
            dve.wait_ge(prep_act, 1)
            dve.wait_ge(prep, PREP_BIAS)

            def centre(L, g, waits):
                d, st = LN[L], stat[L]
                xin = d["x"][g % 2]
                for sm, val in waits:
                    dve.wait_ge(sm, val)
                v.tensor_reduce(st[:, 0, :], xin[:, :, :], AX, ALU.add).then_inc(ln_v[L].sem, 1)
                dve.wait_ge(ln_v[L].sem, ln_v[L].at(g, 1))
                v.scalar_tensor_tensor(out=d["c"][:, :, :], in0=per_tile(st[:, 0, :], d["w"]), scalar=-1.0 / d["w"],
                                       in1=xin[:, :, :], op0=ALU.mult, op1=ALU.add).then_inc(ln_v[L].sem, 1)

            def square_sum(L, g):
                dve.wait_ge(ln_s[L].sem, ln_s[L].at(g))
                v.tensor_reduce(stat[L][:, 1, :], LN[L]["q"][:, :, :], AX, ALU.add).then_inc(ln_v[L].sem, 1)

            def normalise(L, g, waits):
                d = LN[L]
                dve.wait_ge(ln_p[L].sem, ln_p[L].at(g))
                for sm, val in waits:
                    dve.wait_ge(sm, val)
                if L == "c":
                    for q in range(2):
                        t4 = slice(4 * q, 4 * q + 4)
                        v.tensor_tensor(xnrm2[:, t4, :].rearrange("p (k m) c -> p m k c", k=2),
                                        xcen2[:, t4, :].rearrange("p (m k) c -> p m k c", k=2),
                                        stat[L][:, 3, t4].rearrange("p (m k) -> p m k", k=2).unsqueeze(3)
                                        .to_broadcast([P, 2, 2, C]), ALU.mult).then_inc(ln_v[L].sem, 1)
                    return
                v.tensor_tensor(d["n"][:, :, :], d["c"][:, :, :], per_tile(stat[L][:, 3, :], d["w"]), ALU.mult)\
                    .then_inc(ln_v[L].sem, 1)
                dve.wait_ge(ln_v[L].sem, ln_v[L].at(g, 4))
                v.tensor_copy(parts(L)[0], d["n"][:, :, :]).then_inc(ln_v[L].sem, 1)

            def top2(l, g, ps):
                G, S, c = gt[l], gs[l], gv[l]

                def after(k):
                    dve.wait_ge(c.sem, c.at(g, k))

                iota = per_col(iota_m8[:, :], T, E)
                dve.wait_ge(gmm[l].sem, gmm[l].at(g))
                v.scalar_tensor_tensor(out=G[:, 0], in0=ps[:, 0:T * E].rearrange("p (t e) -> p t e", t=T),
                                       scalar=1.0 / WS, in1=per_col(gb[l][:, :], T, E), op0=ALU.mult, op1=ALU.add)\
                    .then_inc(c.sem, 1)
                after(1)
                v.tensor_reduce(S[:, 0], G[:, 0], AX, ALU.max).then_inc(c.sem, 1)
                after(2)
                v.tensor_tensor(G[:, 1], G[:, 0], per_tile(S[:, 0], E), ALU.subtract).then_inc(c.sem, 1)
                after(3)
                v.scalar_tensor_tensor(out=G[:, 3], in0=G[:, 1], scalar=0.0, in1=iota, op0=ALU.is_equal, op1=ALU.mult)\
                    .then_inc(c.sem, 1)
                after(4)
                v.tensor_reduce(S[:, 1], G[:, 3], AX, ALU.min).then_inc(c.sem, 1)
                after(5)
                v.tensor_tensor(G[:, 4], iota, per_tile(S[:, 1], E), ALU.is_equal).then_inc(c.sem, 1)
                after(6)
                v.scalar_tensor_tensor(out=G[:, 5], in0=G[:, 4], scalar=-1e30, in1=G[:, 1], op0=ALU.mult, op1=ALU.add)\
                    .then_inc(c.sem, 1)
                after(7)
                v.tensor_reduce(S[:, 2], G[:, 5], AX, ALU.max).then_inc(c.sem, 1)
                after(8)
                v.tensor_tensor(G[:, 6], G[:, 5], per_tile(S[:, 2], E), ALU.is_equal).then_inc(c.sem, 1)
                after(9)
                v.tensor_tensor(G[:, 7], G[:, 6], iota, ALU.mult).then_inc(c.sem, 1)
                after(10)
                v.tensor_reduce(S[:, 3], G[:, 7], AX, ALU.min).then_inc(c.sem, 1)
                after(11)
                v.tensor_tensor(G[:, 8], iota, per_tile(S[:, 3], E), ALU.is_equal).then_inc(c.sem, 1)
                after(12)
                v.tensor_tensor(G[:, 9], G[:, 4], G[:, 8], ALU.add).then_inc(c.sem, 1)
                after(13)
                dve.wait_ge(ge[l].sem, ge[l].at(g))
                v.tensor_tensor(G[:, 10], G[:, 2], G[:, 9], ALU.mult).then_inc(c.sem, 1)
                after(14)
                v.tensor_reduce(S[:, 4], G[:, 2] if l == 0 else G[:, 10], AX, ALU.add).then_inc(c.sem, 1)
                after(15)
                v.reciprocal(S[:, 5], S[:, 4]).then_inc(c.sem, 1)
                after(16)
                v.tensor_tensor(wgt[l][:, :, :].rearrange("p e t -> p t e"), G[:, 10], per_tile(S[:, 5], E), ALU.mult)\
                    .then_inc(c.sem, 1)

            def ab(g, k):
                if k == 0:
                    waits = [(x_loaded[g % 2], 16 * (g // 2 + 1))]
                    if g >= 1:
                        waits.append((trS["b"].sem, trS["b"].at(g - 1)))
                    centre("a", g, waits)
                elif k == 1:
                    square_sum("a", g)
                elif k == 2:
                    normalise("a", g, [])
                elif k == 8:
                    dve.wait_ge(pjS.sem, pjS.at(g))
                    if g >= 1:
                        dve.wait_ge(kv.sem, kv.at(g - 1))
                    v.tensor_tensor(zdt[:, 0], proj[:, :, PROJ - HEADS:PROJ], per_col(dtb[:, :], T, HEADS), ALU.add)\
                        .then_inc(dtv.sem, 1)
                    dve.wait_ge(dtv.sem, dtv.at(g, 1))
                    v.scalar_tensor_tensor(out=zdt[:, 1], in0=zdt[:, 0], scalar=-1.0, in1=zdt[:, 0], op0=ALU.mult,
                                           op1=ALU.min).then_inc(dtv.sem, 1)
                elif k == 9:
                    dve.wait_ge(dts.sem, dts.at(g))
                    v.scalar_tensor_tensor(out=zdt[:, 4], in0=zdt[:, 0], scalar=0.0, in1=zdt[:, 3], op0=ALU.max,
                                           op1=ALU.add).then_inc(dtv.sem, 1)
                    dve.wait_ge(dtv.sem, dtv.at(g, 3))
                    v.scalar_tensor_tensor(out=zdt[:, 1], in0=zdt[:, 4], scalar=-1.0, in1=per_col(expa[:, :], T, HEADS),
                                           op0=ALU.mult, op1=ALU.mult).then_inc(dtv.sem, 1)
                    dve.wait_ge(dtv.sem, dtv.at(g, 4))
                    v.tensor_tensor(Vs[:, :, :].rearrange("p t (h d) -> p t h d", h=HEADS),
                                    proj[:, :, 0:INNER].rearrange("p t (h d) -> p t h d", h=HEADS),
                                    zdt[:, 1].unsqueeze(3).to_broadcast([P, T, HEADS, HDIM]), ALU.mult)\
                        .then_inc(dtv.sem, 1)
                elif k in (12, 13):
                    hf = k - 12
                    dve.wait_ge(vd.sem, vd.at(g))
                    dve.wait_ge(ymm.sem, ymm.at(g, hf + 1))
                    ys = Yd[:, 4 * hf:4 * hf + 4, :]
                    v.tensor_tensor(ys, sA[:, :].rearrange("p (t n) -> p t n", t=4), ys, ALU.add).then_inc(yv.sem, 1)
                    if hf == 1:
                        waits = [(yv.sem, yv.at(g))]
                        if g >= 1:
                            waits.append((ln_lo["n"].sem, ln_lo["n"].at(g - 1)))
                        centre("n", g, waits)
                elif k == 14:
                    square_sum("n", g)
                elif k == 15:
                    waits = [(trS["n"].sem, trS["n"].at(g - 1))] if g >= 1 else []
                    normalise("n", g, waits)
                elif k == 18:
                    dve.wait_ge(omm.sem, omm.at(g))
                    dve.wait_ge(x0b.sem, x0b.at(g))
                    if g >= 2:
                        dve.wait_ge(fin, 4 * (POS[(0, g - 2)] + 1))
                    v.scalar_tensor_tensor(out=X1[g % 2][:, :, :], in0=sA[:, :].rearrange("p (t c) -> p t c", t=T),
                                           scalar=1.0 / WS, in1=X0b[:, :, :], op0=ALU.mult, op1=ALU.add)\
                        .then_inc(x1v.sem, 1)
                elif k == 19:
                    centre("b", g, [(x1v.sem, x1v.at(g)), (ln_lo["a"].sem, ln_lo["a"].at(g))])
                elif k == 20:
                    square_sum("b", g)
                elif k == 21:
                    normalise("b", g, [(trS["a"].sem, trS["a"].at(g))])
                elif k == 24:
                    top2(0, g, sA)

            def cd(g, k):
                if k == 0:
                    waits = [(fin, 4 * (POS[(0, g)] + 1))]
                    if g >= 1:
                        waits.append((trS["d"].sem, trS["d"].at(g - 1)))
                    centre("c", g, waits)
                elif k == 1:
                    square_sum("c", g)
                elif k == 2:
                    normalise("c", g, [])
                elif k in (4, 5):
                    q = k - 4
                    if q == 0:
                        dve.wait_ge(cmm.sem, cmm.at(g))
                    n = 0
                    for i in range(3):
                        for j in range(3):
                            if (i, j) == (1, 1):
                                continue
                            src = PAD[:, q, i:i + SIDE, j:j + SIDE]
                            if n == 0:
                                base = sC[:, q * PIX:(q + 1) * PIX].rearrange("p (r c) -> p r c", r=SIDE)
                            else:
                                dve.wait_ge(tap.sem, tap.at(g, 8 * q + n))
                                base = nacc[:, q]
                            v.scalar_tensor_tensor(out=nacc[:, q], in0=src, scalar=taps[:, 3 * i + j:3 * i + j + 1],
                                                   in1=base, op0=ALU.mult, op1=ALU.add).then_inc(tap.sem, 1)
                            n += 1
                elif k == 8:
                    dve.wait_ge(utr.sem, utr.at(g))
                    v.tensor_tensor(zc[:, :, :], sC[:, :].rearrange("p (t c) -> p t c", t=T), xnrm2[:, :, :], ALU.mult)\
                        .then_inc(cz.sem, 1)
                    dve.wait_ge(cz.sem, cz.at(g, 1))
                    dve.wait_ge(x2b.sem, x2b.at(g))
                    if g >= 2:
                        dve.wait_ge(fin, 4 * (POS[(1, g - 2)] + 1))
                    for q in range(2):
                        t4 = slice(4 * q, 4 * q + 4)
                        v.tensor_tensor(X3[g % 2][:, t4, :].rearrange("p (m k) c -> p m k c", k=2),
                                        zc[:, t4, :].rearrange("p (k m) c -> p m k c", k=2),
                                        X2b[:, t4, :].rearrange("p (m k) c -> p m k c", k=2), ALU.add)\
                            .then_inc(cz.sem, 1)
                elif k == 10:
                    centre("d", g, [(cz.sem, cz.at(g))])
                elif k == 11:
                    square_sum("d", g)
                elif k == 12:
                    normalise("d", g, [])
                elif k == 15:
                    top2(1, g, sC)

            def moe(m, s):
                l, g = m
                ch = CHUNKS[l]
                n = s - 2 * ch - ch
                if n >= 0 and n % ch == 0 and n // ch < 2 * PAIRS:
                    u = n // ch
                    j, hf = u // 2, u % 2
                    dve.wait_ge(y_ready, 8 * POS[m] + u + 1)
                    if u == 0:
                        dve.wait_ge(w_in[l][g % 2], 32 * (g // 2 + 1))
                    if j == 0:
                        if POS[m] >= 1 and u == 0:
                            dve.wait_ge(fin, 4 * POS[m])
                        dst = ACC[l][:, hf * HALF:(hf + 1) * HALF]
                    else:
                        dst = YW[:, u % 4, :]
                        if POS[m] or j >= 3:
                            dve.wait_ge(summed, 6 * POS[m] + u - 5 if j >= 3 else 6 * POS[m])
                    v.scalar_tensor_tensor(out=dst, in0=yP[hf][:, :], scalar=b2[l][:, j:j + 1],
                                           in1=WB[l][:, j, hf * HALF:(hf + 1) * HALF], op0=ALU.add,
                                           op1=ALU.mult).then_inc(scaled, 1)
                if s == E * ch + 2 * ch + 1:
                    res, dst = (X1, X2) if l == 0 else (X3, X4)
                    if l == 1 and g >= 2:
                        dve.wait_ge(x_stored[g % 2], 16 * (g // 2))
                    if l == 0 and g >= 2:
                        dve.wait_ge(x2b.sem, x2b.at(g - 2))
                    for hf in range(2):
                        dve.wait_ge(ftr, 2 * POS[m] + hf + 1)
                        ps = yP[hf][:, :].rearrange("p (t a c) -> p a t c", t=4, a=2)
                        t4 = slice(4 * hf, 4 * hf + 4)
                        v.tensor_tensor(FINT[:, t4, :], ps[:, 0], res[g % 2][:, t4, :], ALU.add).then_inc(fin, 1)
                        dve.wait_ge(fin, 4 * POS[m] + 2 * hf + 1)
                        v.tensor_tensor(dst[g % 2][:, t4, :], ps[:, 1], FINT[:, t4, :], ALU.add).then_inc(fin, 1)

            walk(moe, ab, cd)


N_LOADS = 16 + 13
PREP_W1_0 = 12
PREP_ALL_ = 17
PREP_ALL = 17
PREP_BIAS = 18

_INS = ["x", "L0_conv_W_in", "L0_conv_dt_bias", "L0_conv_A_log", "L0_conv_D_param", "L0_conv_ln_gamma",
        "L0_conv_ln_beta", "L0_conv_W_out", "L0_ffn_gate_w", "L0_ffn_gate_b", "L0_ffn_W1", "L0_ffn_b1", "L0_ffn_W2",
        "L0_ffn_b2", "L1_conv_gamma_k", "L1_conv_gamma_s", "L1_conv_beta", "L1_conv_beta_outside",
        "L1_conv_gamma_outside", "L1_ffn_Wg", "L1_ffn_bg", "L1_ffn_W1", "L1_ffn_b1", "L1_ffn_W2", "L1_ffn_b2"]


def kernel(**inputs):
    import concourse.bacc as bacc
    from concourse.bass_utils import run_bass_kernel_spmd

    nc = bacc.Bacc("TRN2", target_bir_lowering=False, num_devices=1)
    arrays, args = {}, []
    for name in _INS:
        a = np.ascontiguousarray(inputs[name])
        arrays[f"in_{name}"] = a
        args.append(nc.dram_tensor(f"in_{name}", a.shape, mybir.dt.from_np(a.dtype), kind="ExternalInput").ap())
    shape = (IMAGES, SIDE, SIDE, C)
    args.append(nc.dram_tensor("out_0", shape, F32, kind="ExternalOutput").ap())
    build_metaformer(nc, *args)
    r = run_bass_kernel_spmd(nc, [arrays], core_ids=[0])
    return r.results[0]["out_0"]
```

```python
from contextlib import ExitStack

import numpy as np

import concourse.bass as bass
from concourse import mybir

F32 = mybir.dt.float32
F16 = mybir.dt.float16
ACT = mybir.ActivationFunctionType
ALU = mybir.AluOpType
AX = mybir.AxisListType.X

P = 128
IMAGES, SIDE, C = 32, 16, 64
PIX = SIDE * SIDE
IPG = 4
GROUPS = IMAGES // IPG
TOK = IPG * PIX
T = TOK // P
HALF = TOK // 2
E = 8
PAIRS = E // 2
INNER, STATE, HEADS = 128, 16, 8
HDIM = INNER // HEADS
PROJ = INNER + 2 * STATE + HEADS
CHUNKS = (1, 2)
RING = 8
EXP_LN = "natural_log_exp_and_others"
WS = 16.0


class Count:

    def __init__(self, sem, per):
        self.sem, self.per = sem, per

    def at(self, g, k=None):
        return g * self.per + (self.per if k is None else k)


SLOTS = E * sum(CHUNKS)
LAG = 4
NO_FINAL = (-1, -1, -1, -1)
PE_AT = dict(
    ab=dict(turn_a=12, proj0=17, proj1=19, proj2=20, c_cols=21, state=23, y0=24, y1=26, turn_hi=32,
            turn_lo=34, mix_out=35, turn_b=38, gate=41, send=43),
    cd=dict(turn_c=4, pool0=4, turn_u=11, turn_d=15, gate=16, send=19),
    final=(12, 14, 24, 26))
ACT_AT = dict(
    ab=dict(sums_a=7, turn_a=12, proj0=17, proj1=18, proj2=19, c_cols=21, decay=21, state=23, sums_n=28,
            turn_hi=32, turn_lo=33, sums_b=36, turn_b=37, top2=41, send=42),
    cd=dict(sums_c=1, turn_c=4, norms=9, sums_d=11, turn_d=14, top2=17, send=18),
    final=NO_FINAL)
DVE_AT = dict(
    ab=dict(centre_a=0, sums_a=6, norm_a=10, decay=21, values=22, y0=25, y1=27, centre_n=28, sums_n=29,
            norm_n=30, mix_out=35, centre_b=35, sums_b=36, norm_b=37, top2=41, weights=41),
    cd=dict(centre_c=1, sums_c=1, norm_c=3, pool0=5, pool1=6, pool2=7, pool3=7, turn_u=10, centre_d=10,
            sums_d=12, norm_d=14, top2=17, weights=18),
    final=(12, 13, 24, 27))
POOL_AT = dict(
    ab=dict(sums_a=7, norm_a=9, decay=25, state=26, sums_n=30, norm_n=31, sums_b=34),
    cd=dict(sums_c=1, norm_c=2, scale=8, sums_d=12),
    final=NO_FINAL)
SP_AT = dict(
    ab=dict(decay=22, send=41),
    cd=dict(send=21),
    final=NO_FINAL)
STORE_AT = 36
AB_LEAD = 42


def moe_start(layer, g):
    return SLOTS * (g - 1) if layer == 0 else SLOTS * g + E


def ab_start(g):
    return moe_start(0, g) - AB_LEAD


def cd_start(g):
    return moe_start(0, g) + E * CHUNKS[0] + LAG + 2


def final_slots(layer, g, at):
    m = moe_start(layer, g)
    return m + at["final"][2 * layer], m + at["final"][2 * layer + 1]


def walk(moe, final, ab, cd, at, store=None):
    for slot in range(ab_start(0), moe_start(1, GROUPS - 1) + 2 * SLOTS):
        for g in range(GROUPS):
            for layer in range(2):
                s = slot - moe_start(layer, g)
                if 0 <= s < E * CHUNKS[layer] + LAG + 2:
                    moe((layer, g), s)
        for g in range(GROUPS):
            for layer in (1, 0):
                for half in range(2):
                    if slot == final_slots(layer, g, at)[half]:
                        final((layer, g), half)
            if store and slot == moe_start(1, g) + STORE_AT:
                store(g)
            for stage, start, table in ((ab, ab_start(g), at["ab"]), (cd, cd_start(g), at["cd"])):
                for step, s in table.items():
                    if slot == start + s:
                        stage(g, step)


LOADS = {"in": 4, "out": 4, "experts0": 9, "conv1": 7, "experts1": 7}
PREP = {"in": 3, "out": 7, "bias": 8, "experts0": 12, "experts1": 17}


def build_metaformer(nc, x, W_in, dt_bias, A_log, D_param, ln_gamma, ln_beta, W_out, g0_w, g0_b, m0_W1, m0_b1,
                     m0_W2, m0_b2, gamma_k, gamma_s, beta, beta_out, gamma_out, g1_w, g1_b, m1_W1, m1_b1, m1_W2,
                     m1_b2, out):
    ORDER = sorted(((l, g) for l in range(2) for g in range(GROUPS)), key=lambda m: moe_start(*m))
    POS = {m: n for n, m in enumerate(ORDER)}
    CHUNK_BASE = {}
    n = 0
    for m in ORDER:
        CHUNK_BASE[m] = n
        n += E * CHUNKS[m[0]]

    with ExitStack() as ctx:
        def sb(name, shape, dt=F32):
            return ctx.enter_context(nc.sbuf_tensor(name, shape, dt))

        def psum(name, shape, dt=F32):
            return ctx.enter_context(nc.psum_tensor(name, shape, dt))

        def sem(name):
            return ctx.enter_context(nc.semaphore(name))

        def count(name, per):
            return Count(sem(name), per)

        ident16 = sb("ident16", [P, P], F16)
        ident32 = sb("ident32", [P, P])
        neg_half = sb("neg_half", [P, T])
        iota_m8 = sb("iota_m8", [P, E])
        win_f = sb("win_f", [P, PROJ])
        win = sb("win", [P, 2, PROJ], F16)
        win_c = sb("win_c", [P, 2, 32], F16)
        wout_f = sb("wout_f", [P, C])
        wout_g = sb("wout_g", [P, C])
        wout = sb("wout", [P, 2, C], F16)
        gam_col = sb("gam_col", [P, 1])
        bet_col = sb("bet_col", [P, 1])
        bet_rep = sb("bet_rep", [P, P])
        ones = sb("ones", [P, P])
        out_bias = sb("out_bias", [P, C])
        dtb = sb("dtb", [P, HEADS])
        alog = sb("alog", [P, HEADS])
        expa = sb("expa", [P, HEADS])
        dpar = sb("dpar", [P, HEADS])
        gw_f = [sb(f"gw_f{l}", [P, E]) for l in range(2)]
        gw = [sb(f"gw{l}", [P, 2, E], F16) for l in range(2)]
        gb = [sb(f"gb{l}", [P, E]) for l in range(2)]
        NC = [E * c for c in CHUNKS]
        w1 = [sb(f"w1_{l}", [P, 2, NC[l], P], F16) for l in range(2)]
        w2 = [sb(f"w2_{l}", [P, NC[l], C]) for l in range(2)]
        b1 = [sb(f"b1_{l}", [P, NC[l]]) for l in range(2)]
        b2 = [sb(f"b2_{l}", [P, PAIRS]) for l in range(2)]
        mix = sb("mix", [P, P])
        taps = sb("taps", [P, 9])
        nbias = sb("nbias", [P, 1])
        bo_rep = sb("bo_rep", [P, C])
        go_col = sb("go_col", [P, 1])

        X0 = [sb(f"X0_{i}", [P, T, C]) for i in range(2)]
        X0b = sb("X0b", [P, T, C])
        X1 = [sb(f"X1_{i}", [P, T, C]) for i in range(2)]
        X2 = [sb(f"X2_{i}", [P, T, C]) for i in range(2)]
        X2b = sb("X2b", [P, T, C])
        X3 = [sb(f"X3_{i}", [P, T, C]) for i in range(2)]
        X4 = [sb(f"X4_{i}", [P, T, C]) for i in range(2)]
        FINT = sb("FINT", [P, T, C])
        xcen = sb("xcen", [P, T, C])
        xsq = sb("xsq", [P, T, C])
        xnrm = xcen
        xcen2 = sb("xcen2", [P, T, C])
        xsq2 = sb("xsq2", [P, T, C])
        xnrm2 = sb("xnrm2", [P, T, C])
        xcen_b = sb("xcen_b", [P, T, C])
        xsq_b = sb("xsq_b", [P, T, C])
        xnrm_b = xcen_b
        xsplit_b = sb("xsplit_b", [P, T, 2 * C], F16)
        xsplit = sb("xsplit", [P, T, 2 * C], F16)
        xsplit2 = sb("xsplit2", [P, T, 2 * C], F16)
        stat = {L: sb(f"stat_{L}", [P, 4, T]) for L in "anbcd"}
        xTa = sb("xTa", [P, TOK], F16)
        xT = [[sb(f"xT{l}_{i}", [P, TOK], F16) for i in range(2)] for l in range(2)]
        proj = sb("proj", [P, T, PROJ])
        ctS = sb("ctS", [64, HALF])
        zdt = sb("zdt", [P, 5, T, HEADS])
        Vs = sb("Vs", [P, T, INNER])
        Yd = sb("Yd", [P, T, INNER])
        Yc = sb("Yc", [P, T, INNER])
        Ysq = Vs
        KVs = sb("KVs", [64, 2 * INNER])
        ysplit = sb("ysplit", [P, 2, T, INNER], F16)
        yT = sb("yT", [P, 2, TOK], F16)
        gt = [sb(f"gt{l}", [P, 12, T, E]) for l in range(2)]
        gs = [sb(f"gs{l}", [P, 6, T]) for l in range(2)]
        wgt = [sb(f"wgt{l}", [P, E, T]) for l in range(2)]
        wTs = [sb(f"wTs{l}", [E * T, P]) for l in range(2)]
        WB = [sb(f"WB{l}", [P, PAIRS, TOK]) for l in range(2)]
        H = sb("H", [P, RING, TOK])
        w1_f = H[:, 0:2, :].rearrange("p n h -> p (n h)")
        w1_f1 = H[:, 2:4, :].rearrange("p n h -> p (n h)")
        ACC = [sb(f"ACC{l}", [P, TOK]) for l in range(2)]
        YW = sb("YW", [P, 4, HALF])
        PAD = sb("PAD", [P, 2, SIDE + 2, SIDE + 2])
        nacc = sb("nacc", [P, 2, SIDE, SIDE])
        nlog = nrs = nacc
        nrg = sb("nrg", [P, 2, SIDE, SIDE])
        zc = xsq2
        scratch = [[nc.dram_tensor(f"w_scratch{l}_{i}", [E, TOK], F32).ap() for i in range(2)] for l in range(2)]

        hP = [psum(f"hP{i}", [P, TOK]) for i in range(2)]
        yP = [psum(f"yP{i}", [P, HALF]) for i in range(2)]
        sA = psum("sA", [P, HALF])
        sC = psum("sC", [P, HALF])
        sA16 = sA[:, :].bitcast(F16)
        sC16 = sC[:, :].bitcast(F16)

        loaded = {which: sem(f"loaded_{which}") for which in LOADS}
        w1_loaded = sem("w1_loaded")
        mix_loaded = sem("mix_loaded")
        zeroed = sem("zeroed")
        ident_made = sem("ident_made")
        prep = sem("prep")
        prep_act = sem("prep_act")
        bias_mm = sem("bias_mm")
        x_loaded = [sem(f"x_loaded{i}") for i in range(2)]
        ln_v = {L: count(f"ln_v_{L}", 5) for L in "anbcd"}
        ln_s = {L: count(f"ln_s_{L}", 1) for L in "anbcd"}
        ln_p = {L: count(f"ln_p_{L}", 2) for L in "anbcd"}
        ln_lo = {L: count(f"ln_lo_{L}", 1) for L in "anbd"}
        tr = {L: count(f"tr_{L}", 2 if L == "n" else 1) for L in "anbd"}
        trS = {L: count(f"trS_{L}", 2 if L == "n" else 1) for L in "anbd"}
        pj = count("pj", 3)
        pjS = count("pjS", 3)
        ct = count("ct", 1)
        ctC = count("ctC", 1)
        dtv = count("dtv", 5)
        dts = count("dts", 2)
        vd = count("vd", 1)
        x0b = count("x0b", 1)
        kv = count("kv", 1)
        kvS = count("kvS", 1)
        ymm = count("ymm", 2)
        yv = count("yv", 2)
        omm = count("omm", 1)
        x1v = count("x1v", 1)
        gmm = [count(f"gmm{l}", 1) for l in range(2)]
        GV = 17
        gv = [count(f"gv{l}", GV) for l in range(2)]
        ge = [count(f"ge{l}", 1) for l in range(2)]
        wtr = [count(f"wtr{l}", 1) for l in range(2)]
        wts = [count(f"wts{l}", 1) for l in range(2)]
        w_out = [[sem(f"w_out{l}_{i}") for i in range(2)] for l in range(2)]
        w_in = [[sem(f"w_in{l}_{i}") for i in range(2)] for l in range(2)]
        x2b = count("x2b", 1)
        ctr = count("ctr", 1)
        sqT = count("sqT", 2)
        cmm = count("cmm", 1)
        tap = count("tap", 18 - 2)
        nact = count("nact", 2)
        nsc = count("nsc", 1)
        utr = count("utr", 1)
        cz = count("cz", 3)
        h_ready = sem("h_ready")
        gelu_done = sem("gelu_done")
        y_ready = sem("y_ready")
        scaled = sem("scaled")
        summed = sem("summed")
        ftr = sem("ftr")
        fin = sem("fin")
        x_stored = [sem(f"x_stored{i}") for i in range(2)]

        xd = x.rearrange("(g m) h w c -> g m (h w) c", m=IPG)
        od = out.rearrange("(g m) h w c -> g m (h w) c", m=IPG)

        def ring_free(m, s):
            if s < RING:
                m = ORDER[POS[m] - 1]
                s += E * CHUNKS[m[0]]
            return 8 * POS[m] + 2 * ((s - RING) // (2 * CHUNKS[m[0]])) + 2

        def y_unit(m, s):
            n = s - LAG
            if not 0 <= n < E * CHUNKS[m[0]]:
                return None
            j, r = divmod(n, 2 * CHUNKS[m[0]])
            return (j, *divmod(r, CHUNKS[m[0]]))

        def sums_until(u):
            return 6 * (u // 8) + max(0, u % 8 - 1)

        A_USES = ("turn_a", "proj0", "proj1", "proj2", "c_cols", "state", "y0", "y1", "turn_hi", "turn_lo", "mix_out",
                  "turn_b", "gate", "send")
        C_USES = dict(turn_c="turn_c", pool="pool0", turn_u="turn_u", turn_d="turn_d", gate="gate", send="send")

        def previous(uses):
            uses = sorted(uses, key=lambda u: u[0])
            return {u[1:]: b[1:] for b, u in zip(uses, uses[1:])}

        BEFORE_A = previous((ab_start(g) + PE_AT["ab"][k], k, g) for g in range(GROUPS) for k in A_USES)
        BEFORE_C = previous([(cd_start(g) + PE_AT["cd"][at], k, g) for g in range(GROUPS) for k, at in C_USES.items()]
                            + [(final_slots(l, g, PE_AT)[h] - 0.5, ("fin", l, h), g) for g in range(GROUPS) for l in range(2)
                               for h in range(2)])

        def a_read(name, g):
            if (name, g) not in BEFORE_A:
                return zeroed, 1
            name, g = BEFORE_A[(name, g)]
            count, k = {"turn_a": (trS["a"], 1), "proj0": (pjS, 1), "proj1": (pjS, 2), "proj2": (pjS, 3),
                        "c_cols": (ctC, 1), "state": (kvS, 1), "y0": (yv, 1), "y1": (yv, 2), "turn_hi": (trS["n"], 1),
                        "turn_lo": (trS["n"], 2), "mix_out": (x1v, 1), "turn_b": (trS["b"], 1), "gate": (gv[0], 1),
                        "send": (wts[0], 1)}[name]
            return count.sem, count.at(g, k)

        def c_read(name, g):
            if (name, g) not in BEFORE_C:
                return zeroed, 1
            name, g = BEFORE_C[(name, g)]
            if name[0] == "fin":
                return fin, 4 * POS[(name[1], g)] + 2 * name[2] + 2
            count, k = {"turn_c": (sqT, 2), "pool": (tap, 9), "turn_u": (cz, 1), "turn_d": (trS["d"], 1),
                        "gate": (gv[1], 1), "send": (wts[1], 1)}[name]
            return count.sem, count.at(g, k)

        def grouped(dram, g):
            return dram[g].rearrange("m (p k) c -> p m (k c)", k=2)

        def tiled(ap):
            return ap[:, :, :].rearrange("p (m k) c -> p m (k c)", k=2)

        def per_tile(ap, width):
            return ap.unsqueeze(2).to_broadcast([P, T, width])

        def per_col(ap, n, width):
            return ap.unsqueeze(1).to_broadcast([P, n, width])

        LN = {
            "a": dict(x=X0, c=xcen, q=xsq, n=xnrm, s=xsplit, w=C, eps=1e-6),
            "b": dict(x=X1, c=xcen_b, q=xsq_b, n=xnrm_b, s=xsplit_b, w=C, eps=1e-5),
            "c": dict(x=X2, c=xcen2, q=xsq2, n=xnrm2, s=None, w=C, eps=1e-6),
            "d": dict(x=X3, c=xcen2, q=xsq2, n=xnrm2, s=xsplit2, w=C, eps=1e-5),
            "n": dict(x=(Yd, Yd), c=Yc, q=Ysq, n=Yc, s=None, w=INNER, eps=1e-5),
        }

        def parts(L):
            if L == "n":
                return ysplit[:, 0], ysplit[:, 1]
            s = LN[L]["s"]
            return s[:, :, 0:C], s[:, :, C:2 * C]

        ctx.enter_context(nc.allow_non_contiguous_dma(reason="a few small constants are laid out per channel"))
        block = ctx.enter_context(nc.Block())

        @block.sync
        def _(sp):
            def rep(ap):
                return ap.partition_broadcast(P)

            def both_halves(dst, src):
                return [(dst[half * C:half * C + C], src) for half in range(2)]

            def load(which, pairs):
                assert len(pairs) == LOADS[which]
                for dst, src in pairs:
                    sp.dma_start(dst, src).then_inc(loaded[which], 16)

            sp.dma_start(tiled(X0[0]), grouped(xd, 0)).then_inc(x_loaded[0], 16)
            load("in", both_halves(win_f, W_in) + [(dtb[:, :], rep(dt_bias)), (alog[:, :], rep(A_log))])
            load("out", [(wout_f[:, :], W_out), (gam_col[:, :], ln_gamma.rearrange("(c o) -> c o", o=1)),
                         (bet_col[:, :], ln_beta.rearrange("(c o) -> c o", o=1)), (dpar[:, :], rep(D_param))])
            load("experts0", both_halves(gw_f[0], g0_w) + [(gb[0][:, :], rep(g0_b))] + [
                (w1_f[half * C:half * C + C, 0:NC[0] * P].rearrange("d (e h) -> d e h", e=E),
                 m0_W1.rearrange("e d h -> d e h")) for half in range(2)] + [
                (b1[0][:, :], m0_b1.rearrange("e h -> h e")), (w2[0][:, :, :], m0_W2.rearrange("e h f -> h e f"))] + [
                (b2[0][half * C:half * C + C, :], m0_b2.rearrange("(j a) f -> a f j", a=2)[half])
                for half in range(2)])
            load("conv1", both_halves(taps, gamma_s.rearrange("a b c o -> c (a b o)"))
                 + both_halves(nbias, beta.rearrange("(c o) -> c o", o=1))
                 + both_halves(go_col, gamma_out.rearrange("(c o) -> c o", o=1)) + [(bo_rep[:, :], rep(beta_out))])
            sp.wait_ge(zeroed, 2)
            gk = gamma_k.rearrange("a b i o -> (a b i) o")
            for half in range(2):
                for grp in range(8):
                    r = half * C + grp * 8
                    sp.dma_start(mix[r:r + 8, r:r + 8], gk[:, grp * 8:grp * 8 + 8]).then_inc(mix_loaded, 16)
            load("experts1", both_halves(gw_f[1], g1_w) + [(gb[1][:, :], rep(g1_b)),
                 (b1[1][:, :], m1_b1.rearrange("e (c h) -> h (e c)", h=P)),
                 (w2[1][:, :, :], m1_W2.rearrange("e (c h) f -> h (e c) f", h=P))] + [
                (b2[1][half * C:half * C + C, :], m1_b2.rearrange("(j a) f -> a f j", a=2)[half])
                for half in range(2)])
            for half in range(2):
                sp.dma_start(w1_f1[half * C:half * C + C, :].rearrange("d (e h) -> d e h", e=E),
                             m1_W1.rearrange("e d h -> d e h")).then_inc(w1_loaded, 16)

            def spread_weights(l, g):
                i = g % 2
                sp.wait_ge(wts[l].sem, wts[l].at(g))
                sp.dma_start(scratch[l][i].rearrange("e (t p) -> (e t) p", p=P), wTs[l][:, :]).then_inc(w_out[l][i], 16)
                sp.wait_ge(w_out[l][i], 16 * (g // 2 + 1))
                if g >= 1:
                    sp.wait_ge(scaled, 8 * (POS[(l, g - 1)] + 1))
                for a in range(2):
                    src = scratch[l][i].rearrange("(j a) n -> a j n", a=2)[a]
                    sp.dma_start(WB[l][a * C:a * C + C, :, :], src.partition_broadcast(C)).then_inc(w_in[l][i], 16)

            def ab(g, k):
                if k == "decay" and g + 1 < GROUPS:
                    if g >= 1:
                        sp.wait_ge(x0b.sem, x0b.at(g - 1))
                        sp.wait_ge(ln_v["a"].sem, ln_v["a"].at(g - 1, 2))
                    sp.dma_start(tiled(X0[(g + 1) % 2]), grouped(xd, g + 1)).then_inc(x_loaded[(g + 1) % 2], 16)
                if k == "send":
                    spread_weights(0, g)

            def cd(g, k):
                if k == "send":
                    spread_weights(1, g)

            def moe(m, s):
                pass

            def final(m, half):
                pass

            walk(moe, final, ab, cd, SP_AT)
            for i in range(2):
                sp.wait_ge(x_stored[i], 16 * (GROUPS // 2))


        @block.gpsimd
        def _(pool):
            pool.memset(ident16[:, :], 0.0).then_inc(ident_made, 1)
            pool.memset(ident32[:, :], 0.0).then_inc(ident_made, 1)
            pool.wait_ge(ident_made, 2)
            for m in (ident16, ident32):
                pool.affine_select(out=m[:, :], in_=m[:, :], compare_op=ALU.not_equal, fill=1.0, base=0,
                                   pattern=[[-1, P]], channel_multiplier=1).then_inc(ident_made, 1)

            def variance(L, g):
                d, st = LN[L], stat[L]
                pool.wait_ge(ln_v[L].sem, ln_v[L].at(g, 3))
                if L == "a" and g == 0:
                    pool.wait_ge(zeroed, 5)
                pool.tensor_scalar(st[:, 2, :], st[:, 1, :], 1.0 / d["w"], d["eps"], ALU.mult, ALU.add)\
                    .then_inc(ln_p[L].sem, 1)
                pool.wait_ge(ln_p[L].sem, ln_p[L].at(g, 1))
                pool.tensor_tensor(st[:, 3, :], st[:, 2, :], neg_half[:, :], ALU.pow).then_inc(ln_p[L].sem, 1)

            def lo_part(L, g):
                hi, lo = parts(L)
                pool.wait_ge(ln_v[L].sem, ln_v[L].at(g, 5))
                pool.tensor_tensor(lo, LN[L]["n"][:, :, :], hi, ALU.subtract).then_inc(ln_lo[L].sem, 1)

            def ab(g, k):
                if k == "sums_a":
                    variance("a", g)
                elif k == "norm_a":
                    lo_part("a", g)
                elif k == "decay":
                    pool.wait_ge(pjS.sem, pjS.at(g))
                    if g == 0:
                        pool.wait_ge(loaded["out"], 16 * LOADS["out"])
                    else:
                        pool.wait_ge(ln_v["n"].sem, ln_v["n"].at(g - 1, 2))
                    pool.tensor_tensor(Yd[:, :, :].rearrange("p t (h d) -> p t h d", h=HEADS),
                                       proj[:, :, 0:INNER].rearrange("p t (h d) -> p t h d", h=HEADS),
                                       dpar[:, :].unsqueeze(1).unsqueeze(3).to_broadcast([P, T, HEADS, HDIM]),
                                       ALU.mult).then_inc(vd.sem, 1)
                elif k == "state":
                    if g == 0:
                        pool.wait_ge(prep, PREP["bias"])
                    if g >= 1:
                        pool.wait_ge(x1v.sem, x1v.at(g - 1))
                    pool.wait_ge(x_loaded[g % 2], 16 * (g // 2 + 1))
                    pool.tensor_tensor(X0b[:, :, :], X0[g % 2][:, :, :], per_col(out_bias[:, :], T, C), ALU.add)\
                        .then_inc(x0b.sem, 1)
                elif k == "sums_n":
                    variance("n", g)
                elif k == "norm_n":
                    lo_part("n", g)
                elif k == "sums_b":
                    variance("b", g)

            def cd(g, k):
                if k == "sums_c":
                    variance("c", g)
                elif k == "norm_c":
                    if g >= 1:
                        pool.wait_ge(cz.sem, cz.at(g - 1))
                    pool.wait_ge(fin, 4 * (POS[(0, g)] + 1))
                    if g == 0:
                        pool.wait_ge(loaded["conv1"], 16 * LOADS["conv1"])
                    pool.tensor_tensor(X2b[:, :, :], X2[g % 2][:, :, :], per_col(bo_rep[:, :], T, C), ALU.add)\
                        .then_inc(x2b.sem, 1)
                elif k == "scale":
                    pool.wait_ge(nact.sem, nact.at(g, 2))
                    if g == 0:
                        pool.wait_ge(loaded["conv1"], 16 * LOADS["conv1"])
                    pool.tensor_scalar(nrg[:, :, :, :], nrs[:, :, :, :], go_col[:, 0:1], None, ALU.mult)\
                        .then_inc(nsc.sem, 1)
                elif k == "sums_d":
                    variance("d", g)

            def moe(m, s):
                unit = y_unit(m, s - 2)
                l = m[0]
                if unit and unit[0] >= 1 and unit[2] == CHUNKS[l] - 1:
                    j, hf, _ = unit
                    u = 8 * POS[m] + 2 * j + hf
                    cols = slice(hf * HALF, (hf + 1) * HALF)
                    pool.wait_ge(scaled, u + 1)
                    if j >= 2:
                        pool.wait_ge(summed, sums_until(u - 2))
                    pool.tensor_tensor(ACC[l][:, cols], ACC[l][:, cols], YW[:, u % 4, :], ALU.add).then_inc(summed, 1)

            def final(m, half):
                pass

            def store(g):
                pool.wait_ge(fin, 4 * (POS[(1, g)] + 1))
                pool.dma_start(grouped(od, g), tiled(X4[g % 2])).then_inc(x_stored[g % 2], 16)

            walk(moe, final, ab, cd, POOL_AT, store)

        @block.scalar
        def _(act):
            act.wait_ge(loaded["in"], 16 * LOADS["in"])
            nc.scalar.activation(expa[:, :], alog[:, :], ACT.Exp).then_inc(prep_act, 1)

            tables = [None]

            def exp_ln_tables():
                if tables[0] != EXP_LN:
                    act.preload_act_table_set(EXP_LN)
                    tables[0] = EXP_LN

            def squares(L, g):
                d = LN[L]
                act.wait_ge(ln_v[L].sem, ln_v[L].at(g, 2))
                nc.scalar.activation(d["q"][:, :, :], d["c"][:, :, :], ACT.Square).then_inc(ln_s[L].sem, 1)

            def evacuate_T(L, g, src, dst, k=None):
                act.wait_ge(tr[L].sem, tr[L].at(g, k))
                nc.scalar.activation(dst, src, ACT.Copy).then_inc(trS[L].sem, 1)

            def gate_exp(l, g):
                act.wait_ge(gv[l].sem, gv[l].at(g, 3))
                exp_ln_tables()
                nc.scalar.activation(gt[l][:, 2], gt[l][:, 1], ACT.Exp).then_inc(ge[l].sem, 1)

            def gate_evac(l, g, src):
                act.wait_ge(wtr[l].sem, wtr[l].at(g))
                if g >= 1:
                    act.wait_ge(w_out[l][(g - 1) % 2], 16 * ((g - 1) // 2 + 1))
                nc.scalar.activation(wTs[l][:, :], src[0:E * T, 0:P], ACT.Copy).then_inc(wts[l].sem, 1)

            def ab(g, k):
                if k == "sums_a":
                    squares("a", g)
                elif k == "turn_a":
                    evacuate_T("a", g, sA16, xTa[:, :])
                elif k in ("proj0", "proj1", "proj2"):
                    n = int(k[-1])
                    tiles = slice(3 * n, min(3 * n + 3, T))
                    cols = (tiles.stop - tiles.start) * PROJ
                    act.wait_ge(pj.sem, pj.at(g, n + 1))
                    nc.scalar.activation(proj[:, tiles, :].rearrange("p t n -> p (t n)"), sA[:, 0:cols], ACT.Copy,
                                         scale=1.0 / WS).then_inc(pjS.sem, 1)
                elif k == "c_cols":
                    act.wait_ge(ct.sem, ct.at(g))
                    nc.scalar.activation(ctS[:, :], sA[0:64, :], ACT.Copy, scale=1.0 / WS).then_inc(ctC.sem, 1)
                elif k == "decay":
                    act.wait_ge(dtv.sem, dtv.at(g, 2))
                    exp_ln_tables()
                    nc.scalar.activation(zdt[:, 2], zdt[:, 1], ACT.Exp).then_inc(dts.sem, 1)
                    act.wait_ge(dts.sem, dts.at(g, 1))
                    nc.scalar.activation(zdt[:, 3], zdt[:, 2], ACT.Ln, bias=1.0).then_inc(dts.sem, 1)
                elif k == "state":
                    act.wait_ge(kv.sem, kv.at(g))
                    nc.scalar.activation(KVs[:, :], sA[0:64, 0:2 * INNER], ACT.Copy).then_inc(kvS.sem, 1)
                elif k == "sums_n":
                    squares("n", g)
                elif k in ("turn_hi", "turn_lo"):
                    hl = int(k == "turn_lo")
                    evacuate_T("n", g, sA16, yT[:, hl, :], hl + 1)
                elif k == "sums_b":
                    squares("b", g)
                elif k == "turn_b":
                    if g >= 2:
                        act.wait_ge(h_ready, CHUNK_BASE[(0, g - 2)] + E)
                    evacuate_T("b", g, sA16, xT[0][g % 2][:, :])
                elif k == "top2":
                    gate_exp(0, g)
                elif k == "send":
                    gate_evac(0, g, sA)

            def cd(g, k):
                if k == "sums_c":
                    squares("c", g)
                elif k == "turn_c":
                    act.wait_ge(ctr.sem, ctr.at(g))
                    if g == 0:
                        act.wait_ge(zeroed, 2)
                    for q in range(2):
                        nc.scalar.activation(
                            PAD[:, q, 1:SIDE + 1, 1:SIDE + 1].rearrange("p r (c k) -> p k r c", k=2),
                            sC[:, q * 256:(q + 1) * 256].rearrange("p (k r c) -> p k r c", k=2, c=SIDE // 2),
                            ACT.Square).then_inc(sqT.sem, 1)
                elif k == "norms":
                    act.wait_ge(tap.sem, tap.at(g))
                    exp_ln_tables()
                    nc.scalar.activation(nlog[:, :, :, :], nacc[:, :, :, :], ACT.Ln, bias=nbias[:, 0:1])\
                        .then_inc(nact.sem, 1)
                    act.wait_ge(nact.sem, nact.at(g, 1))
                    nc.scalar.activation(nrs[:, :, :, :], nlog[:, :, :, :], ACT.Exp, scale=-0.5).then_inc(nact.sem, 1)
                elif k == "sums_d":
                    squares("d", g)
                elif k == "turn_d":
                    if g >= 2:
                        act.wait_ge(h_ready, CHUNK_BASE[(1, g - 2)] + 2 * E)
                    evacuate_T("d", g, sC16, xT[1][g % 2][:, :])
                elif k == "top2":
                    gate_exp(1, g)
                elif k == "send":
                    gate_evac(1, g, sC)

            def final(m, half):
                pass

            def moe(m, s):
                l, g = m
                ch = CHUNKS[l]
                if s < E * ch:
                    tables[0] = None
                    n = CHUNK_BASE[m] + s
                    act.wait_ge(h_ready, n + 1)
                    if n == 0:
                        act.wait_ge(prep, PREP["experts1"])
                        act.wait_ge(loaded["experts0"], 16 * LOADS["experts0"])
                    elif m == (1, 0) and s == 0:
                        act.wait_ge(loaded["experts1"], 16 * LOADS["experts1"])
                    if n >= RING:
                        act.wait_ge(y_ready, ring_free(m, s))
                    j, r = s // (2 * ch), s % (2 * ch)
                    c, a = r // 2, r % 2
                    e = 2 * j + a
                    nc.scalar.activation(H[:, s % RING, :], hP[s % 2][:, :], ACT.Gelu,
                                         bias=b1[l][:, e * ch + c:e * ch + c + 1], scale=1.0 / WS)\
                        .then_inc(gelu_done, 1)

            walk(moe, final, ab, cd, ACT_AT)

        @block.tensor
        def _(pe):
            pe.wait_ge(ident_made, 4)

            def transposes16(L, g, dst, src, after, k=None):
                for sm, v in after:
                    pe.wait_ge(sm, v)
                for t in range(T):
                    mm = nc.tensor.transpose(dst[:, t * P:(t + 1) * P], src(t), ident16[:, :])
                mm.then_inc(tr[L].sem, 1)

            def gate_product(l, g, ps, src):
                if g == 0:
                    pe.wait_ge(prep, PREP[f"experts{l}"])
                pe.wait_ge(trS[("b", "d")[l]].sem, trS[("b", "d")[l]].at(g))
                for t in range(T):
                    for s in range(2):
                        mm = nc.tensor.matmul(ps[:, t * E:(t + 1) * E], src[:, t * P:(t + 1) * P], gw[l][:, s, :],
                                              start=(s == 0), stop=(s == 1))
                mm.then_inc(gmm[l].sem, 1)

            def gate_transpose(l, g, ps):
                pe.wait_ge(gv[l].sem, gv[l].at(g))
                nc.tensor.transpose(ps[0:E * T, 0:P], wgt[l][:, :, :], ident32[:, :]).then_inc(wtr[l].sem, 1)

            def ab(g, k):
                if k == "turn_a":
                    after = [a_read(k, g)]
                    transposes16("a", g, sA16, lambda t: xsplit[:, t, :],
                                 after + [(ln_lo["a"].sem, ln_lo["a"].at(g))])
                elif k in ("proj0", "proj1", "proj2"):
                    n = int(k[-1])
                    pe.wait_ge(*a_read(k, g))
                    if k == "proj0" and g == 0:
                        pe.wait_ge(prep, PREP["in"])
                    pe.wait_ge(trS["a"].sem, trS["a"].at(g))
                    for t in range(3 * n, min(3 * n + 3, T)):
                        for s in range(2):
                            mm = nc.tensor.matmul(sA[:, (t - 3 * n) * PROJ:(t - 3 * n + 1) * PROJ],
                                                  xTa[:, t * P:(t + 1) * P], win[:, s, :],
                                                  start=(s == 0), stop=(s == 1))
                    mm.then_inc(pj.sem, 1)
                elif k == "c_cols":
                    pe.wait_ge(*a_read(k, g))
                    for s in range(2):
                        for hf in range(2):
                            mm = nc.tensor.matmul(sA[32 * hf:32 * hf + 32, :], win_c[:, s, :],
                                                  xTa[:, hf * HALF:(hf + 1) * HALF], start=(s == 0), stop=(s == 1))
                    mm.then_inc(ct.sem, 1)
                    if g == 0:
                        pe.wait_ge(prep, PREP["out"])
                        nc.tensor.matmul(sC[:, 0:C], bet_rep[:, :], wout_f[:, :], start=True, stop=True)\
                            .then_inc(bias_mm, 1)
                elif k == "state":
                    pe.wait_ge(*a_read(k, g))
                    pe.wait_ge(ctC.sem, ctC.at(g))
                    pe.wait_ge(dtv.sem, dtv.at(g))
                    for m in range(IPG):
                        b = 32 * (m // 2)
                        for t in range(2):
                            mm = nc.tensor.matmul(sA[b:b + 32, (m % 2) * INNER:(m % 2 + 1) * INNER],
                                                  proj[:, 2 * m + t, INNER:INNER + 2 * STATE], Vs[:, 2 * m + t, :],
                                                  start=(t == 0), stop=(t == 1))
                    mm.then_inc(kv.sem, 1)
                elif k in ("y0", "y1"):
                    hf = int(k[-1])
                    pe.wait_ge(*a_read(k, g))
                    pe.wait_ge(kvS.sem, kvS.at(g))
                    q = slice(32 * hf, 32 * hf + STATE)
                    for t in range(4):
                        mm = nc.tensor.matmul(sA[:, t * INNER:(t + 1) * INNER], ctS[q, t * P:(t + 1) * P],
                                              KVs[q, (t // 2) * INNER:(t // 2 + 1) * INNER], start=True, stop=True)
                    mm.then_inc(ymm.sem, 1)
                elif k in ("turn_hi", "turn_lo"):
                    hl = int(k == "turn_lo")
                    part = ln_lo["n"].at(g) if hl else ln_v["n"].at(g, 5)
                    after = [a_read(k, g), ((ln_lo if hl else ln_v)["n"].sem, part)]
                    transposes16("n", g, sA16, lambda t: ysplit[:, hl, t, :], after)
                elif k == "mix_out":
                    pe.wait_ge(*a_read(k, g))
                    pe.wait_ge(trS["n"].sem, trS["n"].at(g))
                    for t in range(T):
                        for n in range(4):
                            mm = nc.tensor.matmul(sA[:, t * C:(t + 1) * C], yT[:, n // 2, t * P:(t + 1) * P],
                                                  wout[:, n % 2, :], start=(n == 0), stop=(n == 3))
                    mm.then_inc(omm.sem, 1)
                elif k == "turn_b":
                    transposes16("b", g, sA16, lambda t: xsplit_b[:, t, :],
                                 [a_read(k, g), (ln_lo["b"].sem, ln_lo["b"].at(g))])
                elif k == "gate":
                    pe.wait_ge(*a_read(k, g))
                    gate_product(0, g, sA, xT[0][g % 2])
                elif k == "send":
                    pe.wait_ge(*a_read(k, g))
                    gate_transpose(0, g, sA)

            def cd(g, k):
                if k == "turn_c":
                    if g == 0:
                        pe.wait_ge(mix_loaded, 16 * 16)
                    pe.wait_ge(*c_read("turn_c", g))
                    pe.wait_ge(ln_v["c"].sem, ln_v["c"].at(g))
                    for n in range(4):
                        mm = nc.tensor.transpose(sC[:, n * P:(n + 1) * P], xnrm2[:, 2 * n:2 * n + 2, :], ident32[:, :])
                    mm.then_inc(ctr.sem, 1)
                elif k == "pool0":
                    pe.wait_ge(*c_read("pool", g))
                    pe.wait_ge(sqT.sem, sqT.at(g))
                    nc.tensor.matmul(sC[:, :].rearrange("p (q r c) -> p q r c", q=2, r=SIDE), mix[:, :],
                                     PAD[:, :, 1:SIDE + 1, 1:SIDE + 1], start=True, stop=True).then_inc(cmm.sem, 1)
                elif k == "turn_u":
                    pe.wait_ge(*c_read("turn_u", g))
                    pe.wait_ge(nsc.sem, nsc.at(g))
                    for q in range(2):
                        for kk in range(2):
                            src = nrg[:, q, :, :].rearrange("p r c -> p (r c)")[:, kk::2]
                            n = 2 * q + kk
                            mm = nc.tensor.transpose(sC[:, n * P:(n + 1) * P], src, ident32[:, :])
                    mm.then_inc(utr.sem, 1)
                elif k == "turn_d":
                    transposes16("d", g, sC16, lambda t: xsplit2[:, t, :],
                                 [c_read("turn_d", g), (ln_lo["d"].sem, ln_lo["d"].at(g))])
                elif k == "gate":
                    pe.wait_ge(*c_read("gate", g))
                    gate_product(1, g, sC, xT[1][g % 2])
                elif k == "send":
                    pe.wait_ge(*c_read("send", g))
                    gate_transpose(1, g, sC)

            def moe(m, s):
                l, g = m
                ch = CHUNKS[l]
                if s < E * ch:
                    n = CHUNK_BASE[m] + s
                    if s == 0:
                        pe.wait_ge(trS["bd"[l]].sem, trS["bd"[l]].at(g))
                    if n >= 2:
                        pe.wait_ge(gelu_done, n - 1)
                    j, r = s // (2 * ch), s % (2 * ch)
                    c, a = r // 2, r % 2
                    w = (2 * j + a) * ch + c
                    for sp in range(2):
                        for hf in range(2):
                            mm = nc.tensor.matmul(hP[s % 2][:, hf * HALF:(hf + 1) * HALF], w1[l][:, sp, w, :],
                                                  xT[l][g % 2][:, hf * HALF:(hf + 1) * HALF],
                                                  start=(sp == 0), stop=(sp == 1))
                    mm.then_inc(h_ready, 1)
                unit = y_unit(m, s)
                if unit:
                    j, hf, c = unit
                    u = 8 * POS[m] + 2 * j + hf
                    if g == 0 and j == 0 and hf == 0 and c == 0:
                        pe.wait_ge(loaded[f"experts{l}"], 16 * LOADS[f"experts{l}"])
                    pe.wait_ge(gelu_done, CHUNK_BASE[m] + 2 * ch * j + 2 * c + 2)
                    if c == 0 and u >= 2:
                        pe.wait_ge(scaled, u - 1)
                    for a in range(2):
                        mm = nc.tensor.matmul(yP[hf][a * C:(a + 1) * C, :], w2[l][:, (2 * j + a) * ch + c, :],
                                              H[:, (2 * ch * j + 2 * c + a) % RING, hf * HALF:(hf + 1) * HALF],
                                              start=(c == 0), stop=(c == ch - 1))
                    if c == ch - 1:
                        mm.then_inc(y_ready, 1)

            def final(m, half):
                l, g = m
                pe.wait_ge(*c_read(("fin", l, half), g))
                pe.wait_ge(summed, sums_until(8 * POS[m] + 6 + half))
                for t in range(4):
                    col = (4 * half + t) * P
                    mm = nc.tensor.transpose(sC[:, t * P:(t + 1) * P], ACC[l][:, col:col + P], ident32[:, :])
                mm.then_inc(ftr, 1)

            walk(moe, final, ab, cd, PE_AT)

        @block.vector
        def _(dve):
            v = nc.vector
            steps = [0]

            def did(ins):
                ins.then_inc(prep, 1)
                steps[0] += 1

            v.memset(PAD[:, :, :, :], 0.0).then_inc(zeroed, 1)
            v.memset(mix[:, :], 0.0).then_inc(zeroed, 1)
            v.memset(win_c[:, :, :], 0.0).then_inc(zeroed, 1)
            v.memset(ones[:, :], 1.0).then_inc(zeroed, 1)
            v.memset(neg_half[:, :], -0.5).then_inc(zeroed, 1)
            for e in range(E):
                v.memset(iota_m8[:, e:e + 1], float(e - E)).then_inc(zeroed, 1)
            dve.wait_ge(zeroed, 5 + E)

            def split(dst_hi, dst_lo, src):
                did(v.tensor_scalar(dst_hi, src, WS, None, ALU.mult))
                dve.wait_ge(prep, steps[0])
                did(v.scalar_tensor_tensor(out=dst_lo, in0=src, scalar=WS, in1=dst_hi, op0=ALU.mult,
                                           op1=ALU.subtract))

            flat = [w1[l][:, :, :, :].rearrange("p s n h -> p s (n h)") for l in range(2)]

            def prepare(which):
                if which == "in":
                    dve.wait_ge(loaded["in"], 16 * LOADS["in"])
                    split(win[:, 0, :], win[:, 1, :], win_f[:, :])
                    dve.wait_ge(prep, steps[0])
                    did(v.tensor_copy(win_c[:, :, 0:STATE], win[:, :, INNER + STATE:INNER + 2 * STATE]))
                elif which == "out":
                    dve.wait_ge(loaded["out"], 16 * LOADS["out"])
                    did(v.tensor_scalar(wout_g[:, :], wout_f[:, :], gam_col[:, 0:1], None, ALU.mult))
                    did(v.tensor_scalar(bet_rep[:, :], ones[:, :], bet_col[:, 0:1], None, ALU.mult))
                    dve.wait_ge(prep, steps[0])
                    split(wout[:, 0, :], wout[:, 1, :], wout_g[:, :])
                elif which == "bias":
                    dve.wait_ge(bias_mm, 1)
                    did(v.tensor_copy(out_bias[:, :], sC[:, 0:C]))
                elif which == "experts0":
                    dve.wait_ge(loaded["experts0"], 16 * LOADS["experts0"])
                    split(gw[0][:, 0, :], gw[0][:, 1, :], gw_f[0][:, :])
                    split(flat[0][:, 0], flat[0][:, 1], w1_f[:, 0:NC[0] * P])
                elif which == "experts1":
                    dve.wait_ge(loaded["experts1"], 16 * LOADS["experts1"])
                    split(gw[1][:, 0, :], gw[1][:, 1, :], gw_f[1][:, :])
                    dve.wait_ge(w1_loaded, 32)
                    split(flat[1][:, 0], flat[1][:, 1], w1_f1[:, :])
                    dve.wait_ge(loaded["conv1"], 16 * LOADS["conv1"])
                    did(v.tensor_scalar(nbias[:, :], nbias[:, :], 1e-6, None, ALU.add))
                assert steps[0] == PREP[which]

            def centre(L, g, waits):
                d, st = LN[L], stat[L]
                xin = d["x"][g % 2]
                for sm, val in waits:
                    dve.wait_ge(sm, val)
                v.tensor_reduce(st[:, 0, :], xin[:, :, :], AX, ALU.add).then_inc(ln_v[L].sem, 1)
                dve.wait_ge(ln_v[L].sem, ln_v[L].at(g, 1))
                v.scalar_tensor_tensor(out=d["c"][:, :, :], in0=per_tile(st[:, 0, :], d["w"]), scalar=-1.0 / d["w"],
                                       in1=xin[:, :, :], op0=ALU.mult, op1=ALU.add).then_inc(ln_v[L].sem, 1)

            def square_sum(L, g):
                dve.wait_ge(ln_s[L].sem, ln_s[L].at(g))
                v.tensor_reduce(stat[L][:, 1, :], LN[L]["q"][:, :, :], AX, ALU.add).then_inc(ln_v[L].sem, 1)

            def normalise(L, g, waits):
                d = LN[L]
                dve.wait_ge(ln_p[L].sem, ln_p[L].at(g))
                for sm, val in waits:
                    dve.wait_ge(sm, val)
                if L == "c":
                    for q in range(2):
                        t4 = slice(4 * q, 4 * q + 4)
                        v.tensor_tensor(xnrm2[:, t4, :].rearrange("p (k m) c -> p m k c", k=2),
                                        xcen2[:, t4, :].rearrange("p (m k) c -> p m k c", k=2),
                                        stat[L][:, 3, t4].rearrange("p (m k) -> p m k", k=2).unsqueeze(3)
                                        .to_broadcast([P, 2, 2, C]), ALU.mult).then_inc(ln_v[L].sem, 1)
                    return
                v.tensor_tensor(d["n"][:, :, :], d["c"][:, :, :], per_tile(stat[L][:, 3, :], d["w"]), ALU.mult)\
                    .then_inc(ln_v[L].sem, 1)
                dve.wait_ge(ln_v[L].sem, ln_v[L].at(g, 4))
                v.tensor_copy(parts(L)[0], d["n"][:, :, :]).then_inc(ln_v[L].sem, 1)
                if L in "bd":
                    hi, lo = parts(L)
                    dve.wait_ge(ln_v[L].sem, ln_v[L].at(g, 5))
                    v.tensor_tensor(lo, d["n"][:, :, :], hi, ALU.subtract).then_inc(ln_lo[L].sem, 1)

            def top2(l, g, ps):
                G, S, c = gt[l], gs[l], gv[l]

                def after(k):
                    dve.wait_ge(c.sem, c.at(g, k))

                iota = per_col(iota_m8[:, :], T, E)
                dve.wait_ge(gmm[l].sem, gmm[l].at(g))
                v.scalar_tensor_tensor(out=G[:, 0], in0=ps[:, 0:T * E].rearrange("p (t e) -> p t e", t=T),
                                       scalar=1.0 / WS, in1=per_col(gb[l][:, :], T, E), op0=ALU.mult, op1=ALU.add)\
                    .then_inc(c.sem, 1)
                after(1)
                v.tensor_reduce(S[:, 0], G[:, 0], AX, ALU.max).then_inc(c.sem, 1)
                after(2)
                v.tensor_tensor(G[:, 1], G[:, 0], per_tile(S[:, 0], E), ALU.subtract).then_inc(c.sem, 1)
                after(3)
                v.scalar_tensor_tensor(out=G[:, 3], in0=G[:, 1], scalar=0.0, in1=iota, op0=ALU.is_equal, op1=ALU.mult)\
                    .then_inc(c.sem, 1)
                after(4)
                v.tensor_reduce(S[:, 1], G[:, 3], AX, ALU.min).then_inc(c.sem, 1)
                after(5)
                v.tensor_tensor(G[:, 4], iota, per_tile(S[:, 1], E), ALU.is_equal).then_inc(c.sem, 1)
                after(6)
                v.scalar_tensor_tensor(out=G[:, 5], in0=G[:, 4], scalar=-1e30, in1=G[:, 1], op0=ALU.mult, op1=ALU.add)\
                    .then_inc(c.sem, 1)
                after(7)
                v.tensor_reduce(S[:, 2], G[:, 5], AX, ALU.max).then_inc(c.sem, 1)
                after(8)
                v.tensor_tensor(G[:, 6], G[:, 5], per_tile(S[:, 2], E), ALU.is_equal).then_inc(c.sem, 1)
                after(9)
                v.tensor_tensor(G[:, 7], G[:, 6], iota, ALU.mult).then_inc(c.sem, 1)
                after(10)
                v.tensor_reduce(S[:, 3], G[:, 7], AX, ALU.min).then_inc(c.sem, 1)
                after(11)
                v.tensor_tensor(G[:, 8], iota, per_tile(S[:, 3], E), ALU.is_equal).then_inc(c.sem, 1)
                after(12)
                v.tensor_tensor(G[:, 9], G[:, 4], G[:, 8], ALU.add).then_inc(c.sem, 1)

            def gate_weights(l, g):
                G, S, c = gt[l], gs[l], gv[l]

                def after(k):
                    dve.wait_ge(c.sem, c.at(g, k))

                after(13)
                dve.wait_ge(ge[l].sem, ge[l].at(g))
                v.tensor_tensor(G[:, 10], G[:, 2], G[:, 9], ALU.mult).then_inc(c.sem, 1)
                after(14)
                v.tensor_reduce(S[:, 4], G[:, 2] if l == 0 else G[:, 10], AX, ALU.add).then_inc(c.sem, 1)
                after(15)
                v.reciprocal(S[:, 5], S[:, 4]).then_inc(c.sem, 1)
                after(16)
                v.tensor_tensor(wgt[l][:, :, :].rearrange("p e t -> p t e"), G[:, 10], per_tile(S[:, 5], E), ALU.mult)\
                    .then_inc(c.sem, 1)

            def ab(g, k):
                if k == "centre_a":
                    waits = [(x_loaded[g % 2], 16 * (g // 2 + 1))]
                    if g >= 1:
                        waits.append((trS["a"].sem, trS["a"].at(g - 1)))
                    centre("a", g, waits)
                elif k == "sums_a":
                    square_sum("a", g)
                elif k == "norm_a":
                    normalise("a", g, [])
                    if g == 0:
                        prepare("in")
                elif k == "decay":
                    dve.wait_ge(pjS.sem, pjS.at(g))
                    if g == 0:
                        prepare("out")
                    if g >= 1:
                        dve.wait_ge(kv.sem, kv.at(g - 1))
                    v.tensor_tensor(zdt[:, 0], proj[:, :, PROJ - HEADS:PROJ], per_col(dtb[:, :], T, HEADS), ALU.add)\
                        .then_inc(dtv.sem, 1)
                    dve.wait_ge(dtv.sem, dtv.at(g, 1))
                    v.scalar_tensor_tensor(out=zdt[:, 1], in0=zdt[:, 0], scalar=-1.0, in1=zdt[:, 0], op0=ALU.mult,
                                           op1=ALU.min).then_inc(dtv.sem, 1)
                elif k == "values":
                    if g == 0:
                        prepare("bias")
                        dve.wait_ge(prep_act, 1)
                    dve.wait_ge(dts.sem, dts.at(g))
                    v.scalar_tensor_tensor(out=zdt[:, 4], in0=zdt[:, 0], scalar=0.0, in1=zdt[:, 3], op0=ALU.max,
                                           op1=ALU.add).then_inc(dtv.sem, 1)
                    dve.wait_ge(dtv.sem, dtv.at(g, 3))
                    v.scalar_tensor_tensor(out=zdt[:, 1], in0=zdt[:, 4], scalar=-1.0, in1=per_col(expa[:, :], T, HEADS),
                                           op0=ALU.mult, op1=ALU.mult).then_inc(dtv.sem, 1)
                    dve.wait_ge(dtv.sem, dtv.at(g, 4))
                    v.tensor_tensor(Vs[:, :, :].rearrange("p t (h d) -> p t h d", h=HEADS),
                                    proj[:, :, 0:INNER].rearrange("p t (h d) -> p t h d", h=HEADS),
                                    zdt[:, 1].unsqueeze(3).to_broadcast([P, T, HEADS, HDIM]), ALU.mult)\
                        .then_inc(dtv.sem, 1)
                elif k in ("y0", "y1"):
                    hf = int(k[-1])
                    dve.wait_ge(vd.sem, vd.at(g))
                    dve.wait_ge(ymm.sem, ymm.at(g, hf + 1))
                    ys = Yd[:, 4 * hf:4 * hf + 4, :]
                    v.tensor_tensor(ys, sA[:, :].rearrange("p (t n) -> p t n", t=4), ys, ALU.add).then_inc(yv.sem, 1)
                elif k == "centre_n":
                    waits = [(yv.sem, yv.at(g))]
                    if g >= 1:
                        waits.append((ln_lo["n"].sem, ln_lo["n"].at(g - 1)))
                    centre("n", g, waits)
                elif k == "sums_n":
                    square_sum("n", g)
                    if g == 0:
                        prepare("experts0")
                elif k == "norm_n":
                    waits = [(trS["n"].sem, trS["n"].at(g - 1))] if g >= 1 else []
                    normalise("n", g, waits)
                elif k == "mix_out":
                    dve.wait_ge(omm.sem, omm.at(g))
                    dve.wait_ge(x0b.sem, x0b.at(g))
                    if g >= 2:
                        dve.wait_ge(fin, 4 * (POS[(0, g - 2)] + 1))
                    v.scalar_tensor_tensor(out=X1[g % 2][:, :, :], in0=sA[:, :].rearrange("p (t c) -> p t c", t=T),
                                           scalar=1.0 / WS, in1=X0b[:, :, :], op0=ALU.mult, op1=ALU.add)\
                        .then_inc(x1v.sem, 1)
                elif k == "centre_b":
                    waits = [(x1v.sem, x1v.at(g))]
                    if g >= 1:
                        waits.append((trS["b"].sem, trS["b"].at(g - 1)))
                    centre("b", g, waits)
                elif k == "sums_b":
                    square_sum("b", g)
                elif k == "norm_b":
                    normalise("b", g, [])
                elif k == "top2":
                    if g == 0:
                        prepare("experts1")
                    top2(0, g, sA)
                elif k == "weights":
                    gate_weights(0, g)

            def cd(g, k):
                if k == "centre_c":
                    waits = [(fin, 4 * (POS[(0, g)] + 1))]
                    if g >= 1:
                        waits.append((trS["d"].sem, trS["d"].at(g - 1)))
                    centre("c", g, waits)
                elif k == "sums_c":
                    square_sum("c", g)
                elif k == "norm_c":
                    normalise("c", g, [])
                elif k in ("pool0", "pool1", "pool2", "pool3"):
                    q, part = divmod(int(k[-1]), 2)
                    if k == "pool0":
                        dve.wait_ge(cmm.sem, cmm.at(g))
                    neighbours = [(i, j) for i in range(3) for j in range(3) if (i, j) != (1, 1)]
                    for n in range(4 * part, 4 * part + 4):
                        i, j = neighbours[n]
                        if n == 0:
                            base = sC[:, q * PIX:(q + 1) * PIX].rearrange("p (r c) -> p r c", r=SIDE)
                        else:
                            dve.wait_ge(tap.sem, tap.at(g, 8 * q + n))
                            base = nacc[:, q]
                        v.scalar_tensor_tensor(out=nacc[:, q], in0=PAD[:, q, i:i + SIDE, j:j + SIDE],
                                               scalar=taps[:, 3 * i + j:3 * i + j + 1], in1=base, op0=ALU.mult,
                                               op1=ALU.add).then_inc(tap.sem, 1)
                elif k == "turn_u":
                    dve.wait_ge(utr.sem, utr.at(g))
                    v.tensor_tensor(zc[:, :, :], sC[:, :].rearrange("p (t c) -> p t c", t=T), xnrm2[:, :, :], ALU.mult)\
                        .then_inc(cz.sem, 1)
                    dve.wait_ge(cz.sem, cz.at(g, 1))
                    dve.wait_ge(x2b.sem, x2b.at(g))
                    if g >= 2:
                        dve.wait_ge(fin, 4 * (POS[(1, g - 2)] + 1))
                    for q in range(2):
                        t4 = slice(4 * q, 4 * q + 4)
                        v.tensor_tensor(X3[g % 2][:, t4, :].rearrange("p (m k) c -> p m k c", k=2),
                                        zc[:, t4, :].rearrange("p (k m) c -> p m k c", k=2),
                                        X2b[:, t4, :].rearrange("p (m k) c -> p m k c", k=2), ALU.add)\
                            .then_inc(cz.sem, 1)
                elif k == "centre_d":
                    centre("d", g, [(cz.sem, cz.at(g))])
                elif k == "sums_d":
                    square_sum("d", g)
                elif k == "norm_d":
                    normalise("d", g, [])
                elif k == "top2":
                    top2(1, g, sC)
                elif k == "weights":
                    gate_weights(1, g)

            def moe(m, s):
                unit = y_unit(m, s - 1)
                l, g = m
                if unit and unit[2] == CHUNKS[l] - 1:
                    j, hf, _ = unit
                    u = 8 * POS[m] + 2 * j + hf
                    cols = slice(hf * HALF, (hf + 1) * HALF)
                    dve.wait_ge(y_ready, u + 1)
                    if j == 0 and hf == 0:
                        dve.wait_ge(w_in[l][g % 2], 32 * (g // 2 + 1))
                    if j == 0:
                        dst = ACC[l][:, cols]
                        if g >= 1:
                            dve.wait_ge(ftr, 2 * POS[(l, g - 1)] + hf + 1)
                    else:
                        dst = YW[:, u % 4, :]
                        if u >= 4:
                            dve.wait_ge(summed, sums_until(u - 4))
                    v.scalar_tensor_tensor(out=dst, in0=yP[hf][:, :], scalar=b2[l][:, j:j + 1],
                                           in1=WB[l][:, j, cols], op0=ALU.add, op1=ALU.mult).then_inc(scaled, 1)

            def final(m, half):
                l, g = m
                res, dst = (X1, X2) if l == 0 else (X3, X4)
                if l == 1 and g >= 2 and half == 0:
                    dve.wait_ge(x_stored[g % 2], 16 * (g // 2))
                if l == 0 and g >= 2:
                    dve.wait_ge(x2b.sem, x2b.at(g - 2))
                dve.wait_ge(ftr, 2 * POS[m] + half + 1)
                ps = sC[:, :].rearrange("p (t a c) -> p a t c", t=4, a=2)
                t4 = slice(4 * half, 4 * half + 4)
                v.tensor_tensor(FINT[:, t4, :], ps[:, 0], res[g % 2][:, t4, :], ALU.add).then_inc(fin, 1)
                dve.wait_ge(fin, 4 * POS[m] + 2 * half + 1)
                v.tensor_tensor(dst[g % 2][:, t4, :], ps[:, 1], FINT[:, t4, :], ALU.add).then_inc(fin, 1)

            walk(moe, final, ab, cd, DVE_AT)


_INS = ["x", "L0_conv_W_in", "L0_conv_dt_bias", "L0_conv_A_log", "L0_conv_D_param", "L0_conv_ln_gamma",
        "L0_conv_ln_beta", "L0_conv_W_out", "L0_ffn_gate_w", "L0_ffn_gate_b", "L0_ffn_W1", "L0_ffn_b1", "L0_ffn_W2",
        "L0_ffn_b2", "L1_conv_gamma_k", "L1_conv_gamma_s", "L1_conv_beta", "L1_conv_beta_outside",
        "L1_conv_gamma_outside", "L1_ffn_Wg", "L1_ffn_bg", "L1_ffn_W1", "L1_ffn_b1", "L1_ffn_W2", "L1_ffn_b2"]


def kernel(**inputs):
    import concourse.bacc as bacc
    from concourse.bass_utils import run_bass_kernel_spmd

    nc = bacc.Bacc("TRN2", target_bir_lowering=False, num_devices=1)
    arrays, args = {}, []
    for name in _INS:
        a = np.ascontiguousarray(inputs[name])
        arrays[f"in_{name}"] = a
        args.append(nc.dram_tensor(f"in_{name}", a.shape, mybir.dt.from_np(a.dtype), kind="ExternalInput").ap())
    shape = (IMAGES, SIDE, SIDE, C)
    args.append(nc.dram_tensor("out_0", shape, F32, kind="ExternalOutput").ap())
    build_metaformer(nc, *args)
    r = run_bass_kernel_spmd(nc, [arrays], core_ids=[0])
    return r.results[0]["out_0"]
```
